# Optimizing a Trainium2 kernel written in Bass

```python
import numpy as np
import jax
import jax.numpy as jnp

def _softmax(x, axis=-1):
    return jax.nn.softmax(x, axis=axis)

def _gelu(x):
    return jax.nn.gelu(x, approximate=True)

def _silu(x):
    return jax.nn.silu(x)

def _sigmoid(x):
    return jax.nn.sigmoid(x)

def _layernorm(x, axis=-1, eps=1e-05):
    m = jnp.mean(x, axis=axis, keepdims=True)
    v = jnp.var(x, axis=axis, keepdims=True)
    return (x - m) / jnp.sqrt(v + eps)

def _scatter_add(tgt, idx, src, axis=0):
    return tgt.at[idx].add(src)

def _segment_sum(src, seg, n):
    return jax.ops.segment_sum(src, seg, n)
kernel_name = 'mk_flamingo_gated_d1_seqx_r4_ac5af8'

def setup_inputs(seed: int=0):
    np.random.seed(seed)
    _w = jnp.asarray

    def _rec_inputs():
        import jax
        import jax.numpy as jnp
        _rk = jax.random.key(seed)
        x = 0.0002417 + 0.9998 * jax.random.normal(jax.random.fold_in(_rk, 1), (32, 128, 256), jnp.float32)
        _lenS = 128 - jax.random.randint(jax.random.fold_in(_rk, 7), (32,), 0, max(1, 128 // 4) + 1, jnp.int32)
        _lenS2 = 128 - jax.random.randint(jax.random.fold_in(_rk, 8), (32,), 0, max(1, 128 // 4) + 1, jnp.int32)
        _ctx_1024P = jax.random.normal(jax.random.fold_in(_rk, 11), (32, 16, 256), jnp.float32)
        _ctx_1024c = jax.random.dirichlet(jax.random.fold_in(_rk, 511), 0.3 * jnp.ones((16,), jnp.float32), (32, 128))
        _ctx_1024t = jnp.einsum('bsk,bkd->bsd', _ctx_1024c, _ctx_1024P)
        _ctx_1024t = _ctx_1024t * jax.lax.rsqrt(jnp.mean(jnp.square(_ctx_1024t)) + 1e-12) * 0.953939
        ctx_1024 = 7.22013e-05 + 1.00017 * (_ctx_1024t + 0.3 * jax.random.normal(jax.random.fold_in(_rk, 611), (32, 128, 256), jnp.float32))
        _validS = jnp.arange(128)[None, :] < _lenS[:, None]
        _validS2 = jnp.arange(128)[None, :] < _lenS2[:, None]
        _causal = jnp.tril(jnp.ones((128, 128), dtype=bool))
        mask_BxS2_bk1 = jnp.broadcast_to(_validS2[:, :], (32, 128))
        _g = jax.random.normal(jax.random.fold_in(_rk, 9001), (2, 1), jnp.float32)
        _g = jnp.sign(_g) * jnp.maximum(jnp.abs(_g), 1.0) + (_g == 0) * 1.0
        g_xattn = _g[0]
        g_ffn = _g[1]
        return (x, ctx_1024, mask_BxS2_bk1, g_xattn, g_ffn)
    x, ctx_1024, mask_BxS2_bk1, g_xattn, g_ffn = _rec_inputs()

    def _L0_xattn_setup():
        import jax, jax.numpy as jnp
        import numpy as np
        D_MODEL = 256
        NUM_HEADS = 16
        DEPTH = D_MODEL // NUM_HEADS
        B, S = (4, 512)
        NEG_INF = float('-inf')

        def _split_heads(x, b):
            return x.reshape(b, -1, NUM_HEADS, DEPTH).transpose(0, 2, 1, 3)
        key = jax.random.key(seed)
        ks = jax.random.split(key, 12)
        inp = {'value': jax.random.normal(ks[0], (B, S, D_MODEL), jnp.float32), 'key': jax.random.normal(ks[1], (B, S, D_MODEL), jnp.float32), 'query': jax.random.normal(ks[2], (B, S, D_MODEL), jnp.float32), 'key_padding_mask': jnp.arange(S)[None, :] < 3 * S // 4}
        inp['key_padding_mask'] = jnp.broadcast_to(inp['key_padding_mask'], (B, S))
        scale = 1.0 / np.sqrt(D_MODEL)
        inp['Wq'] = jax.random.normal(ks[3], (D_MODEL, D_MODEL), jnp.float32) * scale
        inp['bq'] = jnp.zeros((D_MODEL,), jnp.float32)
        inp['Wk'] = jax.random.normal(ks[4], (D_MODEL, D_MODEL), jnp.float32) * scale
        inp['bk'] = jnp.zeros((D_MODEL,), jnp.float32)
        inp['Wv'] = jax.random.normal(ks[5], (D_MODEL, D_MODEL), jnp.float32) * scale
        inp['bv'] = jnp.zeros((D_MODEL,), jnp.float32)
        inp['Wo'] = jax.random.normal(ks[6], (D_MODEL, D_MODEL), jnp.float32) * scale
        inp['bo'] = jnp.zeros((D_MODEL,), jnp.float32)
        return inp
    _L0_xattn_all = _L0_xattn_setup()
    _L0_xattn_in = {k: v for k, v in _L0_xattn_all.items() if k in ('Wq', 'bq', 'Wk', 'bk', 'Wv', 'bv', 'Wo', 'bo')}
    del _L0_xattn_all

    def _L0_ffn_setup():
        import jax, jax.numpy as jnp
        import numpy as np

        def _bitlinear(x, w_latent):
            scale = jax.lax.stop_gradient(jnp.clip(jnp.mean(jnp.abs(w_latent), axis=1, keepdims=True), 1e-05, None))
            tern = jnp.clip(jnp.round(w_latent / scale), -1.0, 1.0)
            w = w_latent + jax.lax.stop_gradient(tern - w_latent)
            return x @ (w * scale).T
        key = jax.random.key(seed)
        ks = jax.random.split(key, 6)
        dim, hidden, rank = (256, 1024, 16)
        B, S = (4, 1024)
        x = jax.random.normal(ks[0], (B, S, dim), dtype=jnp.float32)
        w_fc = 0.02 * jax.random.normal(ks[1], (hidden, dim), dtype=jnp.float32)
        w_proj = 0.02 * jax.random.normal(ks[2], (dim, hidden), dtype=jnp.float32)
        u = 0.02 * jax.random.normal(ks[3], (hidden, rank), dtype=jnp.float32)
        v = 0.02 * jax.random.normal(ks[4], (rank, dim), dtype=jnp.float32)
        fast_b = jax.random.normal(ks[5], (rank, rank), dtype=jnp.float32)
        gate = jnp.float32(0.05)
        return {'x': x, 'fast_b': fast_b, 'w_fc': w_fc, 'w_proj': w_proj, 'u': u, 'v': v, 'gate': gate}
    _L0_ffn_all = _L0_ffn_setup()
    _L0_ffn_in = {k: v for k, v in _L0_ffn_all.items() if k in ('fast_b', 'w_fc', 'w_proj', 'u', 'v', 'gate')}
    del _L0_ffn_all
    return {'x': x, 'ctx_1024': ctx_1024, 'mask_BxS2_bk1': mask_BxS2_bk1, 'g_xattn': g_xattn, 'g_ffn': g_ffn, 'L0_xattn_Wq': _L0_xattn_in['Wq'], 'L0_xattn_bq': _L0_xattn_in['bq'], 'L0_xattn_Wk': _L0_xattn_in['Wk'], 'L0_xattn_bk': _L0_xattn_in['bk'], 'L0_xattn_Wv': _L0_xattn_in['Wv'], 'L0_xattn_bv': _L0_xattn_in['bv'], 'L0_xattn_Wo': _L0_xattn_in['Wo'], 'L0_xattn_bo': _L0_xattn_in['bo'], 'L0_ffn_fast_b': _L0_ffn_in['fast_b'], 'L0_ffn_w_fc': _L0_ffn_in['w_fc'], 'L0_ffn_w_proj': _L0_ffn_in['w_proj'], 'L0_ffn_u': _L0_ffn_in['u'], 'L0_ffn_v': _L0_ffn_in['v'], 'L0_ffn_gate': _L0_ffn_in['gate']}

def reference(x, ctx_1024, mask_BxS2_bk1, g_xattn, g_ffn, L0_xattn_Wq, L0_xattn_bq, L0_xattn_Wk, L0_xattn_bk, L0_xattn_Wv, L0_xattn_bv, L0_xattn_Wo, L0_xattn_bo, L0_ffn_fast_b, L0_ffn_w_fc, L0_ffn_w_proj, L0_ffn_u, L0_ffn_v, L0_ffn_gate):
    import jax
    import jax.numpy as jnp

    def _L0_xattn_ref(value, key, query, key_padding_mask, Wq, bq, Wk, bk, Wv, bv, Wo, bo):
        import jax, jax.numpy as jnp
        import numpy as np
        D_MODEL = 256
        NUM_HEADS = 16
        DEPTH = D_MODEL // NUM_HEADS
        B, S = (4, 512)
        NEG_INF = float('-inf')

        def _split_heads(x, b):
            return x.reshape(b, -1, NUM_HEADS, DEPTH).transpose(0, 2, 1, 3)
        b = query.shape[0]
        q = _split_heads(query @ Wq + bq, b)
        k = _split_heads(key @ Wk + bk, b)
        v = _split_heads(value @ Wv + bv, b)
        logits = jnp.einsum('bhqd,bhkd->bhqk', q, k) / jnp.sqrt(jnp.asarray(DEPTH, q.dtype))
        logits = jnp.where(key_padding_mask[:, None, None, :], logits, NEG_INF)
        attn = jax.nn.softmax(logits, axis=-1)
        out = jnp.einsum('bhqk,bhkd->bhqd', attn, v)
        out = out.transpose(0, 2, 1, 3).reshape(b, -1, D_MODEL)
        return out @ Wo + bo

    def _L0_ffn_ref(x, fast_b, w_fc, w_proj, u, v, gate):
        import jax, jax.numpy as jnp
        import numpy as np

        def _bitlinear(x, w_latent):
            scale = jax.lax.stop_gradient(jnp.clip(jnp.mean(jnp.abs(w_latent), axis=1, keepdims=True), 1e-05, None))
            tern = jnp.clip(jnp.round(w_latent / scale), -1.0, 1.0)
            w = w_latent + jax.lax.stop_gradient(tern - w_latent)
            return x @ (w * scale).T
        h = _bitlinear(x, w_fc) + gate * (x @ v.T @ fast_b.T @ u.T)
        r = jnp.maximum(h, 0.0)
        return _bitlinear(r * r, w_proj)
    x = x + jnp.tanh(g_xattn[0]) * _L0_xattn_ref(ctx_1024, ctx_1024, _layernorm(x, axis=-1), mask_BxS2_bk1, L0_xattn_Wq, L0_xattn_bq, L0_xattn_Wk, L0_xattn_bk, L0_xattn_Wv, L0_xattn_bv, L0_xattn_Wo, L0_xattn_bo)
    x = x + jnp.tanh(g_ffn[0]) * _L0_ffn_ref(_layernorm(x, axis=-1), L0_ffn_fast_b, L0_ffn_w_fc, L0_ffn_w_proj, L0_ffn_u, L0_ffn_v, L0_ffn_gate)
    return x

_drawn_inputs = setup_inputs


def setup_inputs(seed=0):
    import zlib

    import numpy as np

    out = dict(_drawn_inputs(seed))
    spreads = {'L0_xattn_bq': (0.0, 0.475),
     'L0_xattn_bk': (0.0, 0.8),
     'L0_xattn_bv': (0.0, 0.1),
     'L0_xattn_bo': (0.0, 0.1)}
    factors = {'L0_ffn_fast_b': 8.0, 'L0_ffn_u': 8.0, 'L0_ffn_v': 8.0}
    for name, (base, spread) in spreads.items():
        noise = np.random.default_rng([zlib.crc32(name.encode()), seed]).standard_normal(out[name].shape)
        drawn = base * np.exp(spread * noise) if base else spread * noise
        out[name] = jnp.asarray(drawn.astype(out[name].dtype))
    for name, factor in factors.items():
        out[name] = (out[name] * factor).astype(out[name].dtype)
    return out
```

```python
from contextlib import ExitStack

import concourse.bass as bass
from concourse import mybir

F32 = mybir.dt.float32
F32R = mybir.dt.float32r
BF16 = mybir.dt.bfloat16
ALU = mybir.AluOpType
ACT = mybir.ActivationFunctionType
AX_X = mybir.AxisListType.X

P = 128
SEQS, SEQ, D = 32, 128, 256
HEADS = 16
DEPTH = D // HEADS
HID = 1024
RANK = 16
SEQS_PER_GROUP = 4
GROUPS = SEQS // SEQS_PER_GROUP
TOK = SEQS_PER_GROUP * SEQ
DC = D // P
HC = HID // P
QUARTERS = HEADS // 4
STEPS = SEQS_PER_GROUP * QUARTERS
STRIP = 32
PROB_BUFFERS = 3
MAX_SLOTS = 5
EPS = 1e-5
SCALE_MIN = 1e-5
MASKED = 1e30

K_PARTS = [0, 0, 1, 1, 0, 2]
Q_PARTS = [0, 1, 0, 1, 2, 0]
ROWS_QK = DEPTH * len(K_PARTS)
ROW_MASK = ROWS_QK
ROW_MAX = ROWS_QK + 1
ROWS_S1 = ROWS_QK + 1
ROWS_S2 = ROWS_QK + 4


def schedule(first, last):
    steps = ["Load"]
    down = [] if first else [("Down", n) for n in range(2 * SEQS_PER_GROUP)]
    for s in range(STEPS):
        steps.append(("Max", s))
        if s % 2 == 1 and down:
            steps.append(down.pop(0))
    if not first:
        steps.append("Store")
    steps.append("Shift")
    x_early = [] if last else ["XStats", "XNorm", ("XTurn", 0), ("XTurn", 1), "XCtx"]
    steps += x_early
    steps.append("ShiftLoad")
    fill = {}
    if not last:
        for m in range(2 * DC):
            fill[4 * m + 1] = ("XProj", m)
    tail = {}
    for b in range(SEQS_PER_GROUP):
        for n, name in enumerate(["Evict", "Turn4", "Turn2", "Out", "Norm2", "Turn3"]):
            tail.setdefault(4 * b + 4 + n, []).append((name, b))
    for s in range(STEPS + 7):
        if s < STEPS:
            steps.append(("Exp", s))
        if 1 <= s <= STEPS:
            steps.append(("Mix", s - 1))
        steps += tail.get(s, [])
        if s in fill:
            steps.append(fill[s])
        if s >= STEPS and not last and s - STEPS < SEQS_PER_GROUP:
            steps.append(("XVal", s - STEPS))
    if not last:
        steps.append("XStack")
    steps.append("LowRank")
    steps += [("Up", u) for u in range(HC)]
    return steps


BEFORE = ["XLoad", "XStats", "XNorm", ("XTurn", 0), ("XTurn", 1), "XCtx"] + [("XProj", m) for m in range(2 * DC)] + [
    ("XVal", b) for b in range(SEQS_PER_GROUP)] + ["XStack"]
AFTER = [("Down", n) for n in range(2 * SEQS_PER_GROUP)] + ["Store"]


def walk(engine, stages):
    def turn(g, first=False, last=False):
        for step in schedule(first, last):
            name, arg = step if isinstance(step, tuple) else (step, None)
            if name not in stages:
                continue
            group = g + 1 if name[0] == "X" else g - 1 if name in ("Down", "Store") else g
            stages[name](group) if arg is None else stages[name](group, arg)

    def fixed(steps, g):
        for step in steps:
            name, arg = step if isinstance(step, tuple) else (step, None)
            if name in stages:
                stages[name](g) if arg is None else stages[name](g, arg)

    fixed(BEFORE, 0)
    turn(0, first=True)
    with engine.Fori(1, GROUPS - 1) as g:
        turn(g)
    turn(GROUPS - 1, last=True)
    fixed(AFTER, GROUPS - 1)


def need(engine, sem, count):
    if isinstance(count, int) and count <= 0:
        return
    engine.wait_ge(sem, count)


def build_block(nc, x, ctx_t, mask, g_xattn, g_ffn, wq, bq, wk, bk, wv, bv, wo, bo,
                fast_b_t, w_fc_t, w_proj_t, u_t8, v, gate, out):
    with ExitStack() as stack:
        def sb(name, shape, dt):
            return stack.enter_context(nc.sbuf_tensor(name, shape, dt))

        def psum(name, shape):
            return stack.enter_context(nc.psum_tensor(name, shape, F32))

        def sem(name):
            return stack.enter_context(nc.semaphore(name))

        bank_score = psum("bank_score", [P, 2, 512])
        bank_mix = psum("bank_mix", [P, 512])
        bank_f = psum("bank_f", [P, 2, 512])
        bank_x = psum("bank_x", [P, 512])
        bank_t = psum("bank_t", [P, 2, 512])

        w_hi = sb("w_hi", [P, 4, DC, D], F32R)
        w_lo = sb("w_lo", [P, 4, DC, D], F32R)
        bias_qk = sb("bias_qk", [P, 2, DC], F32)
        bias_v = sb("bias_v", [P, D], F32)
        bias_o = sb("bias_o", [P, D], F32)
        gates = sb("gates", [P, 4], F32)
        fc_tern = sb("fc_tern", [P, DC, HID], F32R)
        fc_scale = sb("fc_scale", [P, HC], F32)
        pj_tern = sb("pj_tern", [P, HC, D], F32R)
        pj_scale = sb("pj_scale", [P, D], F32)
        pj_half = sb("pj_half", [P, 2, D], F32)
        pj_gain = sb("pj_gain", [P, D], F32)
        v_in = sb("v_in", [RANK, D], F32)
        fb_in = sb("fb_in", [RANK, RANK], F32)
        fv = sb("fv", [P, DC, RANK], F32)
        fv_hi = sb("fv_hi", [P, DC, RANK], F32R)
        fv_rows = sb("fv_rows", [P, DC, P // RANK, RANK], F32R)
        u_rows = sb("u_rows", [P, HID], F32R)
        mask_in = sb("mask_in", [GROUPS, TOK], mask.dtype)
        mask_row = sb("mask_row", [GROUPS, TOK], BF16)
        ones = sb("ones", [P, P], F32)
        ident = sb("ident", [P, P], F32)
        ident16 = sb("ident16", [P, P], BF16)
        power = sb("power", [P, SEQS_PER_GROUP], F32)
        eps = sb("eps", [P, SEQS_PER_GROUP], F32)

        x_in = sb("x_in", [P, SEQS_PER_GROUP, D], F32)
        x_stat = sb("x_stat", [P, SEQS_PER_GROUP, 6], F32)
        x_mean = sb("x_mean", [P, SEQS_PER_GROUP, 2], F32)
        x_var = sb("x_var", [P, SEQS_PER_GROUP], F32)
        x_rstd = sb("x_rstd", [P, SEQS_PER_GROUP], F32)
        xt_hi = sb("xt_hi", [P, DC, TOK], F32R)
        xt_lo = sb("xt_lo", [P, DC, TOK], F32R)
        c_in = sb("c_in", [P, DC, TOK], F32)
        ct_hi = sb("ct_hi", [P, DC, TOK], F32R)
        ct_lo = sb("ct_lo", [P, DC, TOK], F32R)
        qk = sb("qk", [P, 2, TOK], F32)
        rest = sb("rest", [P, TOK], F32)
        parts = sb("parts", [P, 2 * DC, 3, TOK], BF16)
        vals = sb("vals", [P, SEQS_PER_GROUP, HEADS, STRIP], F32)
        q_stack = sb("q_stack", [P, HEADS, TOK], BF16)
        k_stack = sb("k_stack", [P, HEADS, TOK], BF16)
        maxima = sb("maxima", [P, SEQS_PER_GROUP, HEADS], F32)
        max_rest = sb("max_rest", [P, SEQS_PER_GROUP, HEADS], F32)
        max_parts = sb("max_parts", [P, SEQS_PER_GROUP, MAX_SLOTS, HEADS], BF16)
        hold = sb("hold", [P, 1], F32)
        max_rows = sb("max_rows", [3 * HEADS, TOK], BF16)
        probs = sb("probs", [P, PROB_BUFFERS, 4, SEQ], F32)
        mix_t = sb("mix_t", [P, 512], F32)
        denom = sb("denom", [P, HEADS], F32)
        attn = sb("attn", [P, D], F32)
        at_hi = sb("at_hi", [P, DC, SEQ], F32R)
        at_lo = sb("at_lo", [P, DC, SEQ], F32R)
        residual = sb("residual", [P, 2, SEQS_PER_GROUP, D], F32)
        res_in, res_bias = residual[:, 0], residual[:, 1]
        x1 = sb("x1", [P, SEQS_PER_GROUP, D], F32)
        n_stat = sb("n_stat", [P, 6], F32)
        n_mean = sb("n_mean", [P, 2], F32)
        n_var = sb("n_var", [P, 1], F32)
        n_rstd = sb("n_rstd", [P, 1], F32)
        x1_norm = sb("x1_norm", [P, D], F32)
        nt_hi = sb("nt_hi", [P, DC, TOK], F32R)
        nt_lo = sb("nt_lo", [P, DC, TOK], F32R)
        low_rows = sb("low_rows", [P, TOK], F32R)
        relu = sb("relu", [P, 2, TOK], F32)
        square = sb("square", [P, 2, TOK], F32)
        sq_hi = sb("sq_hi", [P, HC, TOK], F32R)
        sq_lo = sb("sq_lo", [P, HC, TOK], F32R)
        y = sb("y", [P, 2, D], F32)

        w_in = residual[:, :, :, :].rearrange("p a b (c n) -> p (a b) c n", c=1).rearrange("p (w c) e n -> p w (c e) n", w=4)
        early_q = q_stack[:, :, :].rearrange("p h t -> p (h t)").bitcast(F32)
        early_k = k_stack[:, :, :].rearrange("p h t -> p (h t)").bitcast(F32)
        fc_in = early_q[:, 0:DC * HID].rearrange("p (c n) -> p c n", c=DC)
        pj_in = early_q[:, DC * HID:DC * HID + HC * D].rearrange("p (c n) -> p c n", c=HC)
        half_scale = early_k[:, 0:2 * HID].rearrange("p (a n) -> p a n", a=2)
        scale_row = early_k[:, 2 * HID:3 * HID]
        u_in = early_k[:, 3 * HID:4 * HID]
        fc_abs = parts[:, :, :, :].rearrange("p m n t -> p (m n t)").bitcast(F32)[:, 0:DC * HID].rearrange("p (c n) -> p c n", c=DC)
        pj_abs = vals[:, :, :, :].rearrange("p b h e -> p (b h e)").rearrange("p (c n) -> p c n", c=HC)

        scratch_qk = nc.dram_tensor("scratch_qk", (2, 3, D, TOK), BF16, kind="Internal").ap()
        scratch_max = nc.dram_tensor("scratch_max", (3, HEADS, TOK), BF16, kind="Internal").ap()
        scratch_mask = nc.dram_tensor("scratch_mask", (GROUPS, TOK), BF16, kind="Internal").ap()

        w_loaded = sem("w_loaded")
        fc_loaded = sem("fc_loaded")
        small_loaded = sem("small_loaded")
        mask_loaded = sem("mask_loaded")
        mask_made = sem("mask_made")
        mask_written = sem("mask_written")
        consts_made = sem("consts_made")
        pool_consts = sem("pool_consts")
        w_split = sem("w_split")
        gates_made = sem("gates_made")
        abs_made = sem("abs_made")
        sums_made = sem("sums_made")
        scales_made = sem("scales_made")
        tern_made = sem("tern_made")
        fv_summed = sem("fv_summed")
        low_made = sem("low_made")
        x_loaded = sem("x_loaded")
        c_loaded = sem("c_loaded")
        res_loaded = sem("res_loaded")
        x_counted = sem("x_counted")
        x_averaged = sem("x_averaged")
        x_var_made = sem("x_var_made")
        x_rstd_made = sem("x_rstd_made")
        x_normed = sem("x_normed")
        x_turned = sem("x_turned")
        xt_hi_made = sem("xt_hi_made")
        xt_lo_made = sem("xt_lo_made")
        ct_hi_made = sem("ct_hi_made")
        ct_lo_made = sem("ct_lo_made")
        qk_projected = sem("qk_projected")
        qk_biased = sem("qk_biased")
        part_high = sem("part_high")
        part_rest = sem("part_rest")
        part_low = sem("part_low")
        parts_written = [sem(f"parts_written{m}") for m in range(2 * DC)]
        k_stacked = sem("k_stacked")
        q_stacked = sem("q_stacked")
        v_projected = sem("v_projected")
        vals_made = sem("vals_made")
        s1_done = sem("s1_done")
        max_taken = sem("max_taken")
        max_high = sem("max_high")
        max_rest_made = sem("max_rest_made")
        max_mid = sem("max_mid")
        max_split = sem("max_split")
        max_turned = sem("max_turned")
        max_rows_made = sem("max_rows_made")
        max_written = sem("max_written")
        max_loaded = sem("max_loaded")
        s2_done = sem("s2_done")
        exp_done = sem("exp_done")
        mix_done = sem("mix_done")
        mix_evicted = sem("mix_evicted")
        mix_turned = sem("mix_turned")
        denom_made = sem("denom_made")
        attn_made = sem("attn_made")
        attn_turned = sem("attn_turned")
        at_hi_made = sem("at_hi_made")
        at_lo_made = sem("at_lo_made")
        o_projected = sem("o_projected")
        res_biased = sem("res_biased")
        x1_made = sem("x1_made")
        n_counted = sem("n_counted")
        n_averaged = sem("n_averaged")
        n_var_made = sem("n_var_made")
        n_rstd_made = sem("n_rstd_made")
        x1_normed = sem("x1_normed")
        x1_turned = sem("x1_turned")
        nt_hi_made = sem("nt_hi_made")
        nt_lo_made = sem("nt_lo_made")
        low_summed = sem("low_summed")
        low_hi_made = sem("low_hi_made")
        low_lo_made = sem("low_lo_made")
        up_done = sem("up_done")
        relu_made = sem("relu_made")
        sq_hi_made = sem("sq_hi_made")
        square_made = sem("square_made")
        sq_lo_made = sem("sq_lo_made")
        down_done = sem("down_done")
        y_made = sem("y_made")
        out_made = sem("out_made")
        stored = sem("stored")

        SG = SEQS_PER_GROUP
        W_LOADS, SMALL_LOADS, POOL_CONSTS = 4, 11, 5
        stack_k_loads = len(K_PARTS) + 1
        stack_q_loads = len(Q_PARTS)

        block = stack.enter_context(nc.Block())

        @block.sync
        def _(sp):
            def x_load(g):
                need(sp, x_turned, 2 * g)
                sp.dma_start(x_in[:, :, :], x[bass.ds(SG * g, SG)].rearrange("b p d -> p b d")).then_inc(x_loaded, 16)
                need(sp, ct_lo_made, g)
                sp.dma_start(c_in[:, :, :], ctx_t[:, bass.ds(TOK * g, TOK)].rearrange("(c p) t -> p c t", p=P)
                             ).then_inc(c_loaded, 16)

            def load(g, x_too=True):
                need(sp, res_biased, g)
                sp.dma_start(res_in[:, :, :], x[bass.ds(SG * g, SG)].rearrange("b p d -> p b d")).then_inc(res_loaded, 16)
                if x_too:
                    x_load(g + 1)

            def shift_load(g):
                sp.wait_ge(max_rows_made, g + 1)
                sp.dma_start(scratch_max.rearrange("n h t -> (n h) t"), max_rows[:, :]).then_inc(max_written, 16)
                sp.wait_ge(max_written, 16 * (g + 1))
                sp.dma_start(q_stack[ROW_MAX:ROW_MAX + 3, :, :], scratch_max).then_inc(max_loaded, 16)

            def x_proj(g, m):
                sp.wait_ge(part_low, 2 * DC * g + m + 1)
                sp.dma_start(scratch_qk[m // DC].rearrange("n (c p) t -> c p n t", p=P)[m % DC],
                             parts[:, m, :, :]).then_inc(parts_written[m], 16)

            def x_stack(g):
                need(sp, s2_done, STEPS * g)
                for which, names, tile, done in ((1, K_PARTS, k_stack, k_stacked), (0, Q_PARTS, q_stack, q_stacked)):
                    for c in range(DC):
                        sp.wait_ge(parts_written[DC * which + c], 16 * (g + 1))
                    for n, part in enumerate(names):
                        sp.dma_start(tile[DEPTH * n:DEPTH * (n + 1), :, :],
                                     scratch_qk[which, part].rearrange("(h d) t -> d h t", d=DEPTH)).then_inc(done, 16)
                row = scratch_mask[bass.ds(g, 1)]
                sp.dma_start(k_stack[ROW_MASK:ROW_MASK + 1, :, :], row.unsqueeze(1).to_broadcast([1, HEADS, TOK])
                             ).then_inc(k_stacked, 16)

            def store(g):
                sp.wait_ge(out_made, SG * (g + 1))
                sp.dma_start(out[bass.ds(SG * g, SG)].rearrange("b p d -> p b d"), x1[:, :, :]).then_inc(stored, 16)

            x_load(0)
            for n, w in enumerate((wq, wk, wv, wo)):
                sp.dma_start(w_in[:, n, :, :], w.rearrange("(c p) n -> p c n", p=P)).then_inc(w_loaded, 16)
            for n, b in enumerate((bq, bk)):
                sp.dma_start(bias_qk[:, n, :], b).then_inc(small_loaded, 16)
            for tile, b in ((bias_v, bv), (bias_o, bo)):
                sp.dma_start(tile[:, :], b.partition_broadcast(P)).then_inc(small_loaded, 16)
            for n, s in enumerate((g_xattn, g_ffn, gate)):
                sp.dma_start(gates[:, n:n + 1], s.partition_broadcast(P)).then_inc(small_loaded, 16)
            sp.dma_start(v_in[:, :], v).then_inc(small_loaded, 16)
            sp.dma_start(fb_in[:, :], fast_b_t).then_inc(small_loaded, 16)
            sp.dma_start(u_in[:, :], u_t8).then_inc(small_loaded, 16)
            sp.dma_start(mask_in[:, :], mask.rearrange("(g s) k -> g (s k)", s=SG)).then_inc(small_loaded, 16)
            sp.dma_start(fc_in[:, :, :], w_fc_t.rearrange("(c p) n -> p c n", p=P)).then_inc(fc_loaded, 16)
            sp.dma_start(pj_in[:, :, :], w_proj_t.rearrange("(c p) n -> p c n", p=P)).then_inc(fc_loaded, 16)
            sp.wait_ge(mask_made, 1)
            sp.dma_start(scratch_mask, mask_row[:, :]).then_inc(mask_written, 16)
            sp.wait_ge(consts_made, 2)
            sp.wait_ge(mask_written, 16)

            def load_stage(g):
                load(g, x_too=not (isinstance(g, int) and g == GROUPS - 1))

            walk(sp, {"Load": load_stage, "ShiftLoad": shift_load, "XProj": x_proj, "XStack": x_stack, "Store": store})
            sp.wait_ge(stored, 16 * GROUPS)

        @block.tensor
        def _(pe):
            def split_product(dst, pairs):
                for n, (lhs, rhs) in enumerate(pairs):
                    mm = pe.matmul(dst, lhs, rhs, start=n == 0, stop=n == len(pairs) - 1)
                return mm

            def prepare():
                pe.wait_ge(abs_made, 2)
                pe.wait_ge(consts_made, 1)
                for n in range(2):
                    split_product(bank_f[:, n, :], [(ones[:, :], fc_abs[:, c, n * 512:(n + 1) * 512]) for c in range(DC)])
                split_product(bank_t[:, 0, 0:D], [(ones[:, :], pj_abs[:, c, :]) for c in range(HC)])
                for u in range(HC):
                    mm = split_product(bank_t[:, 1, u:u + 1], [(fc_abs[:, c, u * P:(u + 1) * P], ones[:, 0:1]) for c in range(DC)])
                mm.then_inc(sums_made, 1)
                pe.wait_ge(small_loaded, 16 * SMALL_LOADS)
                for c in range(DC):
                    mm = pe.matmul(bank_mix[:, c * RANK:(c + 1) * RANK], v_in[:, c * P:(c + 1) * P], fb_in[:, :], start=True, stop=True)
                mm.then_inc(fv_summed, 1)

            def x_turn(g, half):
                pe.wait_ge(x_normed, SG * g + 2 * half + 2)
                if half == 0:
                    need(pe, vals_made, SG * g)
                else:
                    pe.wait_ge(xt_lo_made, 2 * g + 1)
                for c in range(DC):
                    for n in range(2):
                        mm = pe.transpose(bank_x[:, (2 * c + n) * P:(2 * c + n + 1) * P],
                                          x_in[:, 2 * half + n, c * P:(c + 1) * P], ident[:, :])
                mm.then_inc(x_turned, 1)

            def x_proj(g, m):
                which, c = m // DC, m % DC
                hi, lo = (xt_hi, xt_lo) if which == 0 else (ct_hi, ct_lo)
                if m == 0:
                    pe.wait_ge(xt_lo_made, 2 * g + 2)
                    need(pe, w_split, 2)
                else:
                    pe.wait_ge(qk_biased, 2 * DC * g + m)
                if m == DC:
                    pe.wait_ge(ct_hi_made, g + 1)
                    pe.wait_ge(ct_lo_made, g + 1)
                cols = slice(c * P, (c + 1) * P)
                split_product(bank_x[:, :], [(w[:, which, k, cols], t[:, k, :])
                                             for w, t in ((w_hi, hi), (w_lo, hi), (w_hi, lo)) for k in range(DC)]
                              ).then_inc(qk_projected, 1)

            def x_val(g, b):
                if b == 0:
                    pe.wait_ge(qk_biased, 2 * DC * (g + 1))
                else:
                    pe.wait_ge(vals_made, SG * g + b)
                toks = slice(b * SEQ, (b + 1) * SEQ)
                split_product(bank_x[:, 0:D], [(t[:, k, toks], w[:, 2, k, :])
                                               for w, t in ((w_hi, ct_hi), (w_lo, ct_hi), (w_hi, ct_lo)) for k in range(DC)]
                              ).then_inc(v_projected, 1)

            def max_scores(g, s):
                b, quarter = s // QUARTERS, s % QUARTERS
                if s == 0:
                    pe.wait_ge(k_stacked, 16 * stack_k_loads * (g + 1))
                    pe.wait_ge(q_stacked, 16 * stack_q_loads * (g + 1))
                if s < 2:
                    need(pe, exp_done, STEPS * g - 1 + s)
                else:
                    pe.wait_ge(max_taken, STEPS * g + s - 1)
                toks = slice(b * SEQ, (b + 1) * SEQ)
                for n in range(4):
                    h = 4 * quarter + n
                    mm = pe.matmul(bank_score[:, s % 2, n * SEQ:(n + 1) * SEQ], q_stack[0:ROWS_S1, h, toks],
                                   k_stack[0:ROWS_S1, h, toks], start=True, stop=True)
                mm.then_inc(s1_done, 1)

            def shift(g):
                pe.wait_ge(max_split, g + 1)
                need(pe, x1_made, SG * g)
                rows = bank_t[0:MAX_SLOTS * HEADS, 0, 0:TOK // 2].bitcast(BF16)
                for b in range(SG):
                    mm = pe.transpose(rows[:, b * SEQ:(b + 1) * SEQ],
                                      max_parts[:, b, :, :].rearrange("p n h -> p (n h)"), ident16[:, :])
                mm.then_inc(max_turned, 1)

            def exp_scores(g, s):
                b, quarter = s // QUARTERS, s % QUARTERS
                if s == 0:
                    pe.wait_ge(max_loaded, 16 * (g + 1))
                if s < 2:
                    pe.wait_ge(max_taken, STEPS * g + STEPS - 1 + s)
                else:
                    pe.wait_ge(exp_done, STEPS * g + s - 1)
                toks = slice(b * SEQ, (b + 1) * SEQ)
                for n in range(4):
                    h = 4 * quarter + n
                    mm = pe.matmul(bank_score[:, s % 2, n * SEQ:(n + 1) * SEQ], k_stack[0:ROWS_S2, h, toks],
                                   q_stack[0:ROWS_S2, h, toks], start=True, stop=True)
                mm.then_inc(s2_done, 1)

            def mix(g, s):
                b, quarter = s // QUARTERS, s % QUARTERS
                pe.wait_ge(exp_done, STEPS * g + s + 1)
                if quarter == 0:
                    pe.wait_ge(vals_made, SG * g + b + 1)
                    need(pe, mix_evicted, SG * g + b)
                for n in range(4):
                    mm = pe.matmul(bank_mix[STRIP * n:STRIP * (n + 1), quarter * SEQ:(quarter + 1) * SEQ],
                                   vals[:, b, 4 * quarter + n, :], probs[:, s % PROB_BUFFERS, n, :], start=True, stop=True)
                mm.then_inc(mix_done, 1)

            def turn4(g, b):
                pe.wait_ge(mix_evicted, SG * g + b + 1)
                if b == 0:
                    pe.wait_ge(max_rows_made, g + 1)
                else:
                    pe.wait_ge(x1_made, SG * g + b)
                for n in range(QUARTERS):
                    mm = pe.transpose(bank_t[:, 0, n * P:(n + 1) * P], mix_t[:, n * P:(n + 1) * P], ident[:, :])
                mm.then_inc(mix_turned, 1)

            def turn2(g, b):
                pe.wait_ge(attn_made, SG * g + b + 1)
                need(pe, nt_lo_made, SG * g + b)
                for c in range(DC):
                    mm = pe.transpose(bank_t[:, 1, c * P:(c + 1) * P], attn[:, c * P:(c + 1) * P], ident[:, :])
                mm.then_inc(attn_turned, 1)

            def out_proj(g, b):
                pe.wait_ge(at_lo_made, SG * g + b + 1)
                split_product(bank_t[:, 0, 0:D], [(t[:, k, :], w[:, 3, k, :])
                                                  for w, t in ((w_hi, at_hi), (w_lo, at_hi), (w_hi, at_lo)) for k in range(DC)]
                              ).then_inc(o_projected, 1)

            def turn3(g, b):
                pe.wait_ge(x1_normed, SG * g + b + 1)
                pe.wait_ge(at_lo_made, SG * g + b + 1)
                for c in range(DC):
                    mm = pe.transpose(bank_t[:, 1, c * P:(c + 1) * P], x1_norm[:, c * P:(c + 1) * P], ident[:, :])
                mm.then_inc(x1_turned, 1)

            def low_rank(g):
                pe.wait_ge(nt_lo_made, SG * (g + 1))
                need(pe, y_made, SG * g)
                need(pe, low_made, 2)
                split_product(bank_f[:, 0, :], [(fv_rows[:, k, :, :].rearrange("p a r -> p (a r)"), t[:, k, :])
                                                for t in (nt_hi, nt_lo) for k in range(DC)]).then_inc(low_summed, 1)

            def up(g, u):
                cols = slice(u * P, (u + 1) * P)
                if u == 1:
                    pe.wait_ge(low_lo_made, g + 1)
                elif u > 1:
                    pe.wait_ge(relu_made, HC * g + u - 1)
                dst = bank_f[:, (u + 1) % 2, :]
                if u == 0:
                    need(pe, tern_made, 2)
                for n, (t, k) in enumerate((t, k) for t in (nt_hi, nt_lo) for k in range(DC)):
                    pe.matmul(dst, fc_tern[:, k, cols], t[:, k, :], start=n == 0, stop=False)
                if u == 0:
                    pe.wait_ge(low_lo_made, g + 1)
                pe.matmul(dst, u_rows[:, cols], low_rows[:, :], start=False, stop=True).then_inc(up_done, 1)

            def down(g, n):
                b, half = n // 2, n % 2
                toks = slice(b * SEQ, (b + 1) * SEQ)
                dst = bank_f[:, (b + 1) % 2, 0:D]
                if n == 0:
                    pe.wait_ge(relu_made, HC * g + HC - 1)
                elif n == 2:
                    pe.wait_ge(relu_made, HC * g + HC)
                elif half == 0:
                    pe.wait_ge(y_made, SG * g + b - 1)
                for u in range(half * HC // 2, (half + 1) * HC // 2):
                    if b == 0:
                        pe.wait_ge(sq_lo_made, HC * g + u + 1)
                        pe.wait_ge(sq_hi_made, HC * g + u + 1)
                    pe.matmul(dst, sq_hi[:, u, toks], pj_tern[:, u, :], start=u == 0, stop=False)
                    mm = pe.matmul(dst, sq_lo[:, u, toks], pj_tern[:, u, :], start=False, stop=u == HC - 1)
                if half == 1:
                    mm.then_inc(down_done, 1)

            pe.wait_ge(pool_consts, POOL_CONSTS)
            prepare()
            walk(pe, {"XTurn": x_turn, "XProj": x_proj, "XVal": x_val, "Max": max_scores, "Shift": shift,
                      "Exp": exp_scores, "Mix": mix, "Turn4": turn4, "Turn2": turn2, "Out": out_proj,
                      "Turn3": turn3, "LowRank": low_rank, "Up": up, "Down": down})

        @block.scalar
        def _(act):
            def x_turn(g, half):
                act.wait_ge(x_turned, 2 * g + half + 1)
                need(act, qk_projected, 2 * DC * g)
                act.activation(xt_hi[:, :, 2 * half * SEQ:2 * (half + 1) * SEQ],
                               bank_x[:, :].rearrange("p (c t) -> p c t", c=DC), ACT.Copy).then_inc(xt_hi_made, 1)

            def x_proj(g, m):
                act.wait_ge(qk_projected, 2 * DC * g + m + 1)
                need(act, part_rest, 2 * DC * g + m - 1)
                act.activation(qk[:, m % 2, :], bank_x[:, :], ACT.Identity,
                               bias=bias_qk[:, m // DC, m % DC:m % DC + 1]).then_inc(qk_biased, 1)

            def shift(g):
                act.wait_ge(max_turned, g + 1)
                need(act, max_written, 16 * g)
                act.activation(max_rows[:, :], bank_t[0:3 * HEADS, 0, 0:TOK // 2].bitcast(BF16), ACT.Copy
                               ).then_inc(max_rows_made, 1)

            def exp_scores(g, s):
                act.wait_ge(s2_done, STEPS * g + s + 1)
                need(act, mix_done, STEPS * g + max(0, s + 1 - PROB_BUFFERS))
                act.activation(probs[:, s % PROB_BUFFERS, :, :].rearrange("p n t -> p (n t)"), bank_score[:, s % 2, :], ACT.Exp,
                               scale=float(DEPTH) ** -0.5).then_inc(exp_done, 1)

            def turn2(g, b):
                act.wait_ge(attn_turned, SG * g + b + 1)
                need(act, o_projected, SG * g + b)
                act.activation(at_hi[:, :, :], bank_t[:, 1, 0:D].rearrange("p (c t) -> p c t", c=DC), ACT.Copy
                               ).then_inc(at_hi_made, 1)

            def turn3(g, b):
                act.wait_ge(x1_turned, SG * g + b + 1)
                if b == 0:
                    need(act, up_done, HC * g)
                act.activation(nt_hi[:, :, b * SEQ:(b + 1) * SEQ], bank_t[:, 1, 0:D].rearrange("p (c t) -> p c t", c=DC),
                               ACT.Copy).then_inc(nt_hi_made, 1)

            def low_rank(g):
                act.wait_ge(low_summed, g + 1)
                need(act, up_done, HC * g)
                act.activation(low_rows[:, :], bank_f[:, 0, :], ACT.Copy).then_inc(low_hi_made, 1)

            def up(g, u):
                act.wait_ge(up_done, HC * g + u + 1)
                need(act, square_made, HC * g + u - 1)
                act.activation(relu[:, u % 2, :], bank_f[:, (u + 1) % 2, :], ACT.Relu, scale=fc_scale[:, u:u + 1]
                               ).then_inc(relu_made, 1)
                act.wait_ge(relu_made, HC * g + u + 1)
                if u == 0:
                    need(act, down_done, SG * g)
                act.activation(sq_hi[:, u, :], relu[:, u % 2, :], ACT.Square).then_inc(sq_hi_made, 1)

            act.wait_ge(small_loaded, 16 * SMALL_LOADS)
            act.activation(gates[:, 0:2], gates[:, 0:2], ACT.Tanh).then_inc(gates_made, 1)
            act.wait_ge(fc_loaded, 32)
            act.activation(fc_abs[:, :, :], fc_in[:, :, :], ACT.Abs).then_inc(abs_made, 1)
            act.activation(pj_abs[:, :, :], pj_in[:, :, :], ACT.Abs).then_inc(abs_made, 1)
            walk(act, {"XTurn": x_turn, "XProj": x_proj, "Shift": shift, "Exp": exp_scores, "Turn2": turn2,
                       "Turn3": turn3, "LowRank": low_rank, "Up": up})

        @block.vector
        def _(dve):
            def prepare_attention():
                dve.memset(max_parts[:, :, :, :], 0.0)
                dve.memset(ones[:, :], 1.0).then_inc(consts_made, 1)
                dve.wait_ge(small_loaded, 16 * SMALL_LOADS)
                dve.tensor_scalar(mask_row[:, :], mask_in[:, :], MASKED, MASKED, ALU.mult, ALU.subtract).then_inc(mask_made, 1)
                dve.wait_ge(w_loaded, 16 * W_LOADS)
                dve.wait_ge(gates_made, 1)
                dve.tensor_scalar(w_in[:, 3, :, :], w_in[:, 3, :, :], gates[:, 0:1], None, ALU.mult).then_inc(w_split, 1)
                dve.tensor_scalar(bias_o[:, :], bias_o[:, :], gates[:, 0:1], None, ALU.mult).then_inc(gates_made, 1)
                dve.wait_ge(w_split, 1)
                dve.tensor_copy(w_hi[:, :, :, :], w_in[:, :, :, :]).then_inc(tern_made, 1)
                dve.wait_ge(tern_made, 1)
                dve.tensor_tensor(w_lo[:, :, :, :], w_in[:, :, :, :], w_hi[:, :, :, :].bitcast(F32), ALU.subtract
                                  ).then_inc(w_split, 1)

            def prepare_ffn():
                dve.wait_ge(fc_loaded, 32)
                dve.wait_ge(sums_made, 1)
                dve.tensor_scalar(scale_row[:, :], bank_f[:, :, :].rearrange("p a n -> p (a n)"), 1.0 / D, SCALE_MIN,
                                  ALU.mult, ALU.max).then_inc(scales_made, 1)
                dve.tensor_scalar(fc_scale[:, :], bank_t[:, 1, 0:HC], 1.0 / D, SCALE_MIN, ALU.mult, ALU.max
                                  ).then_inc(scales_made, 1)
                dve.tensor_scalar(pj_scale[:, :], bank_t[:, 0, 0:D], 1.0 / HID, SCALE_MIN, ALU.mult, ALU.max
                                  ).then_inc(scales_made, 1)
                dve.wait_ge(scales_made, 3)
                for n, sign in enumerate((0.5, -0.5)):
                    dve.tensor_scalar(half_scale[:, n, :], scale_row[:, :], sign, None, ALU.mult).then_inc(scales_made, 1)
                    dve.tensor_scalar(pj_half[:, n, :], pj_scale[:, :], sign, None, ALU.mult).then_inc(scales_made, 1)
                dve.tensor_scalar(pj_gain[:, :], pj_scale[:, :], gates[:, 1:2], None, ALU.mult).then_inc(scales_made, 1)
                dve.wait_ge(scales_made, 8)
                for c in range(DC):
                    dve.tensor_tensor(fc_abs[:, c, :], fc_in[:, c, :], half_scale[:, 1, :], ALU.is_lt)
                    dve.tensor_tensor(fc_in[:, c, :], fc_in[:, c, :], half_scale[:, 0, :], ALU.is_gt)
                for c in range(HC):
                    dve.tensor_tensor(pj_abs[:, c, :], pj_in[:, c, :], pj_half[:, 1, :], ALU.is_lt)
                    last = dve.tensor_tensor(pj_in[:, c, :], pj_in[:, c, :], pj_half[:, 0, :], ALU.is_gt)
                last.then_inc(scales_made, 1)
                dve.wait_ge(scales_made, 9)
                dve.tensor_tensor(fc_tern[:, :, :], fc_in[:, :, :], fc_abs[:, :, :], ALU.subtract)
                dve.tensor_tensor(pj_tern[:, :, :], pj_in[:, :, :], pj_abs[:, :, :], ALU.subtract).then_inc(tern_made, 1)
                dve.wait_ge(fv_summed, 1)
                dve.tensor_copy(fv[:, :, :], bank_mix[:, 0:DC * RANK].rearrange("p (c r) -> p c r", c=DC)).then_inc(scales_made, 1)
                dve.reciprocal(half_scale[:, 0, :], scale_row[:, :]).then_inc(scales_made, 1)
                dve.tensor_scalar(u_in[:, :], u_in[:, :], gates[:, 2:3], None, ALU.mult).then_inc(scales_made, 1)
                dve.wait_ge(scales_made, 12)
                dve.tensor_copy(fv_hi[:, :, :], fv[:, :, :]).then_inc(scales_made, 1)
                dve.tensor_tensor(half_scale[:, 1, :], u_in[:, :], half_scale[:, 0, :], ALU.mult).then_inc(scales_made, 1)
                dve.wait_ge(scales_made, 14)
                for a in range(0, P // RANK, 2):
                    dve.tensor_copy(fv_rows[:, :, a, :], fv_hi[:, :, :].bitcast(F32))
                    dve.tensor_tensor(fv_rows[:, :, a + 1, :], fv[:, :, :], fv_hi[:, :, :].bitcast(F32), ALU.subtract)
                dve.tensor_copy(u_rows[:, :], half_scale[:, 1, :]).then_inc(low_made, 1)
                dve.wait_ge(low_made, 1)
                for q in (1, 3):
                    rows = slice(32 * q, 32 * (q + 1))
                    last = dve.tensor_tensor(u_rows[rows, :], half_scale[rows, 1, :], u_rows[rows, :].bitcast(F32), ALU.subtract)
                last.then_inc(low_made, 1)
                dve.wait_ge(low_made, 2)
                dve.memset(vals[:, :, :, :], 1.0)
                dve.memset(q_stack[ROWS_QK:P, :, :], 1.0)
                dve.memset(k_stack[ROWS_QK:P, :, :], 1.0).then_inc(consts_made, 1)

            def x_stats(g):
                dve.wait_ge(x_loaded, 16 * (g + 1))
                need(dve, x_rstd_made, g)
                for b in range(SG):
                    last = dve.bn_stats(x_stat[:, b, :], x_in[:, b, :])
                last.then_inc(x_counted, 1)
                dve.wait_ge(x_counted, g + 1)
                dve.memset(hold[:, :], 0.0)
                for b in range(SG):
                    last = dve.bn_aggr(x_mean[:, b, :], x_stat[:, b, :])
                last.then_inc(x_averaged, 1)

            def x_normalise(g):
                dve.wait_ge(x_rstd_made, g + 1)
                for b in range(SG):
                    dve.tensor_scalar(x_in[:, b, :], x_in[:, b, :], x_mean[:, b, 0:1], x_rstd[:, b:b + 1],
                                      ALU.subtract, ALU.mult).then_inc(x_normed, 1)

            def x_turn(g, half):
                dve.wait_ge(xt_hi_made, 2 * g + half + 1)
                cols = slice(2 * half * SEQ, 2 * (half + 1) * SEQ)
                dve.tensor_tensor(xt_lo[:, :, cols], bank_x[:, :].rearrange("p (c t) -> p c t", c=DC),
                                  xt_hi[:, :, cols].bitcast(F32), ALU.subtract).then_inc(xt_lo_made, 1)

            def x_ctx(g):
                dve.wait_ge(c_loaded, 16 * (g + 1))
                need(dve, v_projected, SG * g)
                dve.tensor_copy(ct_hi[:, :, :], c_in[:, :, :]).then_inc(ct_hi_made, 1)

            def x_proj(g, m):
                dve.wait_ge(qk_biased, 2 * DC * g + m + 1)
                need(dve, parts_written[m], 16 * g)
                dve.tensor_copy(parts[:, m, 0, :], qk[:, m % 2, :]).then_inc(part_high, 1)

            def x_val(g, b):
                dve.wait_ge(v_projected, SG * g + b + 1)
                need(dve, mix_done, STEPS * (g - 1) + QUARTERS * (b + 1))
                dve.tensor_tensor(vals[:, b, :, 0:DEPTH], bank_x[:, 0:D].rearrange("p (h d) -> p h d", h=HEADS),
                                  bias_v[:, :].rearrange("p (h d) -> p h d", h=HEADS), ALU.add).then_inc(vals_made, 1)

            def take_max(g, s):
                b, quarter = s // QUARTERS, s % QUARTERS
                dve.wait_ge(s1_done, STEPS * g + s + 1)
                dve.tensor_reduce(maxima[:, b, 4 * quarter:4 * quarter + 4],
                                  bank_score[:, s % 2, :].rearrange("p (n k) -> p n k", n=4), AX_X, ALU.max
                                  ).then_inc(max_taken, 1)

            def shift(g):
                dve.wait_ge(max_taken, STEPS * (g + 1))
                need(dve, max_turned, g)
                dve.tensor_scalar(max_parts[:, :, 0, :], maxima[:, :, :], -1.0, None, ALU.mult).then_inc(max_high, 1)
                dve.wait_ge(max_high, g + 1)
                dve.scalar_tensor_tensor(max_rest[:, :, :], maxima[:, :, :], -1.0, max_parts[:, :, 0, :], ALU.mult,
                                         ALU.subtract).then_inc(max_rest_made, 1)
                dve.wait_ge(max_rest_made, g + 1)
                dve.tensor_copy(max_parts[:, :, 1, :], max_rest[:, :, :]).then_inc(max_mid, 1)
                dve.wait_ge(max_mid, g + 1)
                dve.tensor_tensor(max_parts[:, :, 2, :], max_rest[:, :, :], max_parts[:, :, 1, :], ALU.subtract
                                  ).then_inc(max_split, 1)

            def evict(g, b):
                dve.wait_ge(mix_done, STEPS * g + QUARTERS * (b + 1))
                need(dve, mix_turned, SG * g + b)
                dve.tensor_copy(mix_t[:, :], bank_mix[:, :]).then_inc(mix_evicted, 1)

            def turn4(g, b):
                heads = bank_t[:, 0, :].rearrange("p (h e) -> p h e", h=HEADS)
                dve.wait_ge(mix_turned, SG * g + b + 1)
                dve.reciprocal(denom[:, :], heads[:, :, DEPTH]).then_inc(denom_made, 1)
                dve.wait_ge(denom_made, SG * g + b + 1)
                need(dve, attn_turned, SG * g + b)
                dve.tensor_tensor(attn[:, :].rearrange("p (h d) -> p h d", h=HEADS), heads[:, :, 0:DEPTH],
                                  denom[:, :].unsqueeze(2).to_broadcast([P, HEADS, DEPTH]), ALU.mult).then_inc(attn_made, 1)

            def turn2(g, b):
                dve.wait_ge(at_hi_made, SG * g + b + 1)
                dve.tensor_tensor(at_lo[:, :, :], bank_t[:, 1, 0:D].rearrange("p (c t) -> p c t", c=DC),
                                  at_hi[:, :, :].bitcast(F32), ALU.subtract).then_inc(at_lo_made, 1)

            def out_proj(g, b):
                dve.wait_ge(o_projected, SG * g + b + 1)
                dve.wait_ge(res_biased, g + 1)
                need(dve, stored, 16 * g)
                dve.tensor_tensor(x1[:, b, :], bank_t[:, 0, 0:D], res_bias[:, b, :], ALU.add).then_inc(x1_made, 1)
                dve.wait_ge(x1_made, SG * g + b + 1)
                dve.bn_stats(n_stat[:, :], x1[:, b, :]).then_inc(n_counted, 1)
                dve.wait_ge(n_counted, SG * g + b + 1)
                need(dve, n_rstd_made, SG * g + b)
                dve.memset(hold[:, :], 0.0)
                dve.bn_aggr(n_mean[:, :], n_stat[:, :]).then_inc(n_averaged, 1)

            def norm2(g, b):
                dve.wait_ge(n_rstd_made, SG * g + b + 1)
                need(dve, x1_turned, SG * g + b)
                dve.tensor_scalar(x1_norm[:, :], x1[:, b, :], n_mean[:, 0:1], n_rstd[:, 0:1], ALU.subtract, ALU.mult
                                  ).then_inc(x1_normed, 1)

            def turn3(g, b):
                dve.wait_ge(nt_hi_made, SG * g + b + 1)
                toks = slice(b * SEQ, (b + 1) * SEQ)
                dve.tensor_tensor(nt_lo[:, :, toks], bank_t[:, 1, 0:D].rearrange("p (c t) -> p c t", c=DC),
                                  nt_hi[:, :, toks].bitcast(F32), ALU.subtract).then_inc(nt_lo_made, 1)

            def low_rank(g):
                dve.wait_ge(low_hi_made, g + 1)
                dve.tensor_tensor(low_rows[64:P, :], bank_f[64:P, 0, :], low_rows[64:P, :].bitcast(F32), ALU.subtract
                                  ).then_inc(low_lo_made, 1)

            def up(g, u):
                dve.wait_ge(square_made, HC * g + u + 1)
                dve.wait_ge(sq_hi_made, HC * g + u + 1)
                dve.tensor_tensor(sq_lo[:, u, :], square[:, u % 2, :], sq_hi[:, u, :].bitcast(F32), ALU.subtract
                                  ).then_inc(sq_lo_made, 1)

            def down(g, n):
                if n % 2 == 0:
                    return
                b = n // 2
                dve.wait_ge(down_done, SG * g + b + 1)
                if b >= 2:
                    dve.wait_ge(out_made, SG * g + b - 1)
                dve.tensor_tensor(y[:, b % 2, :], bank_f[:, (b + 1) % 2, 0:D], pj_gain[:, :], ALU.mult).then_inc(y_made, 1)

            prepare_attention()
            prepare_ffn()
            walk(dve, {"XStats": x_stats, "XNorm": x_normalise, "XTurn": x_turn, "XCtx": x_ctx, "XProj": x_proj,
                       "XVal": x_val, "Max": take_max, "Shift": shift, "Evict": evict, "Turn4": turn4, "Turn2": turn2,
                       "Out": out_proj, "Norm2": norm2, "Turn3": turn3, "LowRank": low_rank, "Up": up, "Down": down})

        @block.gpsimd
        def _(pool):
            def x_stats(g):
                pool.wait_ge(x_averaged, g + 1)
                pool.tensor_tensor(x_var[:, :], x_mean[:, :, 1], eps[:, :], ALU.add).then_inc(x_var_made, 1)
                pool.wait_ge(x_var_made, g + 1)
                need(pool, x_normed, SG * g)
                pool.tensor_tensor(x_rstd[:, :], x_var[:, :], power[:, :], ALU.pow).then_inc(x_rstd_made, 1)

            def x_ctx(g):
                pool.wait_ge(ct_hi_made, g + 1)
                pool.tensor_tensor(ct_lo[:, :, :], c_in[:, :, :], ct_hi[:, :, :].bitcast(F32), ALU.subtract
                                   ).then_inc(ct_lo_made, 1)

            def x_proj(g, m):
                pool.wait_ge(part_high, 2 * DC * g + m + 1)
                pool.tensor_tensor(parts[:, m, 1, :], qk[:, m % 2, :], parts[:, m, 0, :], ALU.subtract)
                need(pool, part_low, 2 * DC * g + m)
                pool.tensor_tensor(rest[:, :], qk[:, m % 2, :], parts[:, m, 0, :], ALU.subtract).then_inc(part_rest, 1)
                pool.wait_ge(part_rest, 2 * DC * g + m + 1)
                pool.tensor_tensor(parts[:, m, 2, :], rest[:, :], parts[:, m, 1, :], ALU.subtract
                                   ).then_inc(part_low, 1)

            def shift(g):
                pool.wait_ge(res_loaded, 16 * (g + 1))
                need(pool, x1_made, SG * g)
                for b in range(SG):
                    last = pool.tensor_tensor(res_bias[:, b, :], res_in[:, b, :], bias_o[:, :], ALU.add)
                last.then_inc(res_biased, 1)

            def out_proj(g, b):
                pool.wait_ge(n_averaged, SG * g + b + 1)
                pool.tensor_tensor(n_var[:, :], n_mean[:, 1:2], eps[:, 0:1], ALU.add).then_inc(n_var_made, 1)
                pool.wait_ge(n_var_made, SG * g + b + 1)
                need(pool, x1_normed, SG * g + b)
                pool.tensor_tensor(n_rstd[:, :], n_var[:, :], power[:, 0:1], ALU.pow).then_inc(n_rstd_made, 1)

            def up(g, u):
                pool.wait_ge(relu_made, HC * g + u + 1)
                need(pool, sq_lo_made, HC * g + u - 1)
                pool.tensor_tensor(square[:, u % 2, :], relu[:, u % 2, :], relu[:, u % 2, :], ALU.mult
                                   ).then_inc(square_made, 1)

            def down(g, n):
                if n % 2 == 0:
                    return
                b = n // 2
                pool.wait_ge(y_made, SG * g + b + 1)
                pool.tensor_tensor(x1[:, b, :], y[:, b % 2, :], x1[:, b, :], ALU.add).then_inc(out_made, 1)

            pool.memset(power[:, :], -0.5)
            pool.memset(eps[:, :], EPS).then_inc(pool_consts, 1)
            pool.memset(ident[:, :], 0.0).then_inc(pool_consts, 1)
            pool.memset(ident16[:, :], 0.0).then_inc(pool_consts, 1)
            pool.wait_ge(pool_consts, 3)
            for tile in (ident, ident16):
                pool.affine_select(out=tile[:, :], in_=tile[:, :], compare_op=ALU.not_equal, fill=1.0, base=0,
                                   pattern=[[-1, P]], channel_multiplier=1).then_inc(pool_consts, 1)
            pool.wait_ge(pool_consts, POOL_CONSTS)
            pool.wait_ge(gates_made, 2)
            walk(pool, {"XStats": x_stats, "XCtx": x_ctx, "XProj": x_proj, "Shift": shift, "Out": out_proj,
                        "Up": up, "Down": down})


def kernel(**inputs):
    import numpy as np
    import concourse.bacc as bacc
    from concourse.bass_utils import run_bass_kernel_spmd

    def laid_out(a):
        return np.ascontiguousarray(a)

    take = {name: np.asarray(a) for name, a in inputs.items()}
    arrays = {
        "x": take["x"],
        "ctx_t": take["ctx_1024"].reshape(SEQS * SEQ, D).T,
        "mask": take["mask_BxS2_bk1"],
        "g_xattn": take["g_xattn"],
        "g_ffn": take["g_ffn"],
        "wq": take["L0_xattn_Wq"], "bq": take["L0_xattn_bq"].reshape(DC, P).T,
        "wk": take["L0_xattn_Wk"], "bk": take["L0_xattn_bk"].reshape(DC, P).T,
        "wv": take["L0_xattn_Wv"], "bv": take["L0_xattn_bv"],
        "wo": take["L0_xattn_Wo"], "bo": take["L0_xattn_bo"],
        "fast_b_t": take["L0_ffn_fast_b"].T,
        "w_fc_t": take["L0_ffn_w_fc"].T,
        "w_proj_t": take["L0_ffn_w_proj"].T,
        "u_t8": np.tile(take["L0_ffn_u"].T, (P // RANK, 1)),
        "v": take["L0_ffn_v"],
        "gate": take["L0_ffn_gate"].reshape(1),
    }
    nc = bacc.Bacc("TRN2", target_bir_lowering=False, num_devices=1)
    feed, args = {}, {}
    for name, a in arrays.items():
        a = laid_out(a)
        feed[f"in_{name}"] = a
        args[name] = nc.dram_tensor(f"in_{name}", a.shape, mybir.dt.from_np(a.dtype), kind="ExternalInput").ap()
    args["out"] = nc.dram_tensor("out_x", (SEQS, SEQ, D), F32, kind="ExternalOutput").ap()
    build_block(nc, **args)
    result = run_bass_kernel_spmd(nc, [feed], core_ids=[0])
    return result.results[0]["out_x"]
```

```python
from contextlib import ExitStack

import concourse.bass as bass
from concourse import mybir

F32 = mybir.dt.float32
F32R = mybir.dt.float32r
BF16 = mybir.dt.bfloat16
ALU = mybir.AluOpType
ACT = mybir.ActivationFunctionType
AX_X = mybir.AxisListType.X

P = 128
SEQS, SEQ, D = 32, 128, 256
HEADS = 16
DEPTH = D // HEADS
HID = 1024
RANK = 16
SG = 4
GROUPS = SEQS // SG
TOK = SG * SEQ
DC = D // P
HC = HID // P
QUARTERS = HEADS // 4
STEPS = SG * QUARTERS
STRIP = 32
PROB_BUFFERS = 3
MIX_LAG = 2
LAST_TAIL = (("Turn4", 0), ("Norm4", 0), ("Turn2", 1), ("Turn2Low", 2), ("Out", 3), ("OutSum", 3))
STATS2_AT, NORM2_AT, TURN3_AT, LOW_RANK_AT = 3, 5, (6, 7), 8
LOAD_AT, BIAS_AT = 7, 14
X_CTX_AT, X_STATS_AT, X_NORM_AT = 5, 11, 14
UP_AT = (9, 10, 11, 12, 13, 14, 15, 16)
UP_LAG = 1
X_TURN_AT = (16, 17)
X_PROJ_AT = (3, 5, 7, 9)
X_VAL_AT = (11, 13, 15)
STACK0_AT = 13
DOWN_AT = (2, 3, 5, 8, 11, 13, 15, 17)
TAIL_LAGS = (("Evict", 0), ("Turn4", 1), ("Norm4", 1), ("Turn2", 2), ("Turn2Low", 3), ("Out", 4), ("OutSum", 4))
EXP_STEPS = STEPS + MIX_LAG
MAX_SLOTS = 5
EPS = 1e-5
SCALE_MIN = 1e-5
MASKED = 1e30

K_PARTS = [0, 0, 1, 1, 0, 2]
Q_PARTS = [0, 1, 0, 1, 2, 0]
ROWS_QK = DEPTH * len(K_PARTS)
ROW_MASK = ROWS_QK
ROW_MAX = ROWS_QK + 1
ROWS_S1 = ROWS_QK + 1
ROWS_S2 = ROWS_QK + 4


def schedule(first, last):
    at = [[] for _ in range(STEPS + EXP_STEPS)]

    def put(slot, distance, name, *arg):
        if not (first and distance < 0 or last and distance > 0):
            at[slot].append((distance, name, *arg))

    for name, slot in LAST_TAIL:
        put(slot, -1, name, SG - 1)
    put(0, 0, "XVal", SG - 1)
    put(1, 0, "XValSum", SG - 1)
    for name, slot in (("Stats2", STATS2_AT), ("Norm2", NORM2_AT), ("Keep", NORM2_AT)):
        put(slot, -1, name)
    for half, slot in enumerate(TURN3_AT):
        put(slot, -1, "Turn3", half)
        put(slot + 1, -1, "Turn3Low", half)
    put(LOW_RANK_AT, -1, "LowRank")
    put(LOW_RANK_AT + 1, -1, "LowRankLow")
    put(LOAD_AT, 0, "Load")
    put(0, 1, "XLoad")
    put(X_CTX_AT, 1, "XCtx")
    put(X_STATS_AT, 1, "XStats")
    put(X_NORM_AT, 1, "XNorm")
    put(STEPS // 2, 0, "Shift", 0)
    put(STEPS // 2 + 1, 0, "ShiftTurn", 0)
    put(STEPS - 1, 0, "Shift", 1)
    put(BIAS_AT, 0, "Bias")
    if first:
        put(STEPS - 1, 0, "Prepare")
    put(STEPS + 1, 0, "ShiftTurn", 1)
    for u, slot in enumerate(UP_AT):
        put(slot, -1, "Up", u)
        put(slot + UP_LAG, -1, "UpLow", u)
    for half, slot in enumerate(X_TURN_AT):
        put(slot, 1, "XTurn", half)
        put(slot + 1, 1, "XTurnLow", half)
    for m, slot in enumerate(X_PROJ_AT):
        put(STEPS + slot, 1, "XProj", m)
        put(STEPS + slot + 1, 1, "XParts", m)
    for b, slot in enumerate(X_VAL_AT):
        put(STEPS + slot, 1, "XVal", b)
        put(STEPS + slot + 1, 1, "XValSum", b)
    for b in range(SG - 1):
        for name, lag in TAIL_LAGS:
            put(STEPS + QUARTERS * (b + 1) + MIX_LAG - 1 + lag, 0, name, b)
    put(STEPS + QUARTERS * SG + MIX_LAG - 1, 0, "Evict", SG - 1)
    for n, slot in enumerate(DOWN_AT):
        put(STEPS + slot, -1, "Down", n)
        if n % 2 == 1:
            put(min(STEPS + slot + 1, len(at) - 1), -1, "Gain", n // 2)
    put(STEPS + STACK0_AT, 1, "XStack", 0)
    put(len(at) - 1, -1, "Store")
    put(len(at) - 1, 1, "XStack", 1)

    steps = []
    for s in range(len(at)):
        if s < STEPS:
            steps.append((0, "Max", s))
        elif s < 2 * STEPS:
            steps.append((0, "Exp", s - STEPS))
        if 0 <= s - STEPS - MIX_LAG < STEPS:
            steps.append((0, "Mix", s - STEPS - MIX_LAG))
        steps += at[s]
    return steps


def stages_x0():
    turns = [step for half in range(2) for step in (("XTurn", half), ("XTurnLow", half))]
    projections = [[("XProj", m), ("XParts", m)] for m in range(2 * DC)]
    values = [step for b in range(SG - 1) for step in (("XVal", b), ("XValSum", b))]
    return [("XStats",), ("XNorm",), ("Weights", 0), *turns, ("XCtx",), *projections[0], *projections[1],
            ("Weights", 1), *projections[2], *projections[3], *values, ("XStack", 0), ("XStack", 1), ("LoadF",)]


def stages_last():
    ups = [step for u in range(HC) for step in (("Up", u), ("UpLow", u))]
    downs = [step for b in range(SG) for step in (("Down", 2 * b), ("Down", 2 * b + 1), ("Gain", b))]
    return [("Turn4", SG - 1), ("Norm4", SG - 1), ("Turn2", SG - 1), ("Turn2Low", SG - 1), ("Out", SG - 1), ("OutSum", SG - 1),
            ("Stats2",), ("Norm2",), ("Keep",), ("Turn3", 0), ("Turn3", 1), ("Turn3Low", 0), ("Turn3Low", 1), ("LowRank",),
            ("LowRankLow",), *ups, *downs, ("Store",)]


def walk(engine, stages):
    def turn(g, first=False, last=False):
        for distance, name, *arg in schedule(first, last):
            if name in stages:
                stages[name](g + distance, *arg)

    for name, *arg in stages_x0():
        if name in stages:
            stages[name](0, *arg)
    turn(0, first=True)
    with engine.Fori(1, GROUPS - 1) as g:
        turn(g)
    turn(GROUPS - 1, last=True)
    for name, *arg in stages_last():
        if name in stages:
            stages[name](GROUPS - 1, *arg)


def need(engine, sem, count):
    if isinstance(count, int) and count <= 0:
        return
    engine.wait_ge(sem, count)


def build_block(nc, x, ctx_t, mask, g_xattn, g_ffn, wq, bq, wk, bk, wv, bv, wo, bo,
                fast_b_t, w_fc_t, w_proj_t, u_t8, v, gate, out):
    with ExitStack() as stack:
        def sb(name, shape, dt):
            return stack.enter_context(nc.sbuf_tensor(name, shape, dt))

        def psum(name, shape):
            return stack.enter_context(nc.psum_tensor(name, shape, F32))

        def sem(name):
            return stack.enter_context(nc.semaphore(name))

        bank_score = psum("bank_score", [P, 2, 512])
        bank_mix = psum("bank_mix", [P, 512])
        bank_f = psum("bank_f", [P, 2, 512])
        bank_x = psum("bank_x", [P, 512])
        bank_t = psum("bank_t", [P, 2, 512])

        w_hi = sb("w_hi", [P, 4, DC, D], F32R)
        w_lo = sb("w_lo", [P, 4, DC, D], F32R)
        bias_qk = sb("bias_qk", [P, 2, DC], F32)
        bias_v = sb("bias_v", [P, D], F32)
        bias_o = sb("bias_o", [P, D], F32)
        gates = sb("gates", [P, 4], F32)
        fc_tern = sb("fc_tern", [P, DC, HID], F32R)
        fc_scale = sb("fc_scale", [P, HC], F32)
        pj_tern = sb("pj_tern", [P, HC, D], F32R)
        pj_scale = sb("pj_scale", [P, D], F32)
        pj_half = sb("pj_half", [P, D], F32)
        pj_gain = sb("pj_gain", [P, D], F32)
        v_in = sb("v_in", [RANK, D], F32)
        fb_in = sb("fb_in", [RANK, RANK], F32)
        fv = sb("fv", [P, DC, RANK], F32)
        fv_hi = sb("fv_hi", [P, DC, RANK], F32R)
        fv_rows = sb("fv_rows", [P, DC, P // RANK, RANK], F32R)
        u_rows = sb("u_rows", [P, HID], F32R)
        mask_in = sb("mask_in", [GROUPS, TOK], mask.dtype)
        mask_row = sb("mask_row", [GROUPS, TOK], BF16)
        ones = sb("ones", [P, P], F32)
        ident = sb("ident", [P, P], F32)
        ident16 = sb("ident16", [P, P], BF16)
        power = sb("power", [P, SG], F32)
        eps = sb("eps", [P, SG], F32)

        x_in = sb("x_in", [P, SG, D], F32)
        x_stat = sb("x_stat", [P, SG, 6], F32)
        x_mean = sb("x_mean", [P, SG, 2], F32)
        x_var = sb("x_var", [P, SG], F32)
        x_rstd = sb("x_rstd", [P, SG], F32)
        xt_hi = sb("xt_hi", [P, DC, TOK], F32R)
        xt_lo = sb("xt_lo", [P, DC, TOK], F32R)
        c_in = sb("c_in", [P, DC, TOK], F32)
        ct_hi = sb("ct_hi", [P, DC, TOK], F32R)
        ct_lo = sb("ct_lo", [P, DC, TOK], F32R)
        qk = sb("qk", [P, 2, TOK], F32)
        rest = sb("rest", [P, TOK], F32)
        parts = sb("parts", [P, 2 * DC, 3, TOK], BF16)
        vals = sb("vals", [P, SG, HEADS, STRIP], F32)
        q_stack = sb("q_stack", [P, HEADS, TOK], BF16)
        k_stack = sb("k_stack", [P, HEADS, TOK], BF16)
        maxima = sb("maxima", [P, SG, HEADS], F32)
        max_rest = sb("max_rest", [P, SG, HEADS], F32)
        max_parts = sb("max_parts", [P, SG, MAX_SLOTS, HEADS], BF16)
        hold = sb("hold", [P, 1], F32)
        max_rows = sb("max_rows", [3 * HEADS, TOK], BF16)
        probs = sb("probs", [P, PROB_BUFFERS, 4, SEQ], F32)
        mix_t = sb("mix_t", [P, 512], F32)
        denom = sb("denom", [P, HEADS], F32)
        attn = sb("attn", [P, D], F32)
        at_hi = sb("at_hi", [P, DC, SEQ], F32R)
        at_lo = sb("at_lo", [P, DC, SEQ], F32R)
        x1_and_norm = sb("x1_and_norm", [P, 2, SG, D], F32)
        x1, x1_norm = x1_and_norm[:, 0], x1_and_norm[:, 1]
        kept = sb("kept", [P, SG, D], F32)
        n_stat = sb("n_stat", [P, SG, 6], F32)
        n_mean = sb("n_mean", [P, SG, 2], F32)
        n_var = sb("n_var", [P, SG], F32)
        n_rstd = sb("n_rstd", [P, SG], F32)
        with ExitStack() as early:
            def early_sb(name, shape):
                return early.enter_context(nc.sbuf_tensor(name, shape, F32))

            fc_in = early_sb("fc_in", [P, DC, HID])
            pj_in = early_sb("pj_in", [P, HC, D])
            fc_abs = early_sb("fc_abs", [P, DC, HID])
            pj_abs = early_sb("pj_abs", [P, HC, D])
            half_scale = early_sb("half_scale", [P, 2, HID])
            scale_row = early_sb("scale_row", [P, HID])
            u_in = early_sb("u_in", [P, HID])
        sq_hi = sb("sq_hi", [P, HC, TOK], F32R)
        sq_lo = sb("sq_lo", [P, HC, TOK], F32R)
        nt_hi = sb("nt_hi", [P, DC, TOK], F32R)
        nt_lo = sb("nt_lo", [P, DC, TOK], F32R)
        relu = sb("relu", [P, 2, TOK], F32)
        square = sb("square", [P, 2, TOK], F32)
        low_rows = sb("low_rows", [P, TOK], F32R)
        y = sb("y", [P, 2, D], F32)
        w_in = x1_and_norm[:, :, :, :].rearrange("p a (w c) n -> p (a w) c n", c=DC)

        scratch_qk = nc.dram_tensor("scratch_qk", (2, 3, D, TOK), BF16, kind="Internal").ap()
        scratch_max = nc.dram_tensor("scratch_max", (3, HEADS, TOK), BF16, kind="Internal").ap()
        scratch_mask = nc.dram_tensor("scratch_mask", (GROUPS, TOK), BF16, kind="Internal").ap()

        w_loaded = [sem("wq_wk_loaded"), sem("wv_wo_loaded")]
        fc_loaded = sem("fc_loaded")
        small_loaded = sem("small_loaded")
        low_loaded = sem("low_loaded")
        mask_loaded = sem("mask_loaded")
        mask_made = sem("mask_made")
        mask_written = sem("mask_written")
        consts_made = sem("consts_made")
        pool_consts = sem("pool_consts")
        wo_gated = sem("wo_gated")
        w_high = sem("w_high")
        w_split = sem("w_split")
        gates_made = sem("gates_made")
        abs_made = sem("abs_made")
        sums_made = sem("sums_made")
        signs_made = sem("signs_made")
        sums_read = sem("sums_read")
        over_half = sem("over_half")
        scales_made = sem("scales_made")
        tern_made = sem("tern_made")
        low_made = sem("low_made")
        x_loaded = sem("x_loaded")
        c_loaded = sem("c_loaded")
        res_loaded = sem("res_loaded")
        x_counted = sem("x_counted")
        x_averaged = sem("x_averaged")
        x_var_made = sem("x_var_made")
        x_rstd_made = sem("x_rstd_made")
        x_normed = sem("x_normed")
        x_turned = sem("x_turned")
        xt_hi_made = sem("xt_hi_made")
        xt_lo_made = sem("xt_lo_made")
        ct_hi_made = sem("ct_hi_made")
        ct_lo_made = sem("ct_lo_made")
        qk_projected = sem("qk_projected")
        qk_biased = sem("qk_biased")
        part_high = sem("part_high")
        part_rest = sem("part_rest")
        part_low = sem("part_low")
        parts_written = [sem(f"parts_written{m}") for m in range(2 * DC)]
        k_stacked = [sem(f"k_stacked{half}") for half in range(2)]
        q_stacked = [sem(f"q_stacked{half}") for half in range(2)]
        v_projected = sem("v_projected")
        vals_made = sem("vals_made")
        s1_done = sem("s1_done")
        max_taken = sem("max_taken")
        max_high = sem("max_high")
        max_rest_made = sem("max_rest_made")
        max_mid = sem("max_mid")
        max_split = sem("max_split")
        max_turned = sem("max_turned")
        max_rows_made = sem("max_rows_made")
        max_written = [sem(f"max_written{half}") for half in range(2)]
        max_loaded = [sem(f"max_loaded{half}") for half in range(2)]
        s2_done = sem("s2_done")
        exp_done = sem("exp_done")
        mix_done = sem("mix_done")
        mix_evicted = sem("mix_evicted")
        mix_turned = sem("mix_turned")
        denom_made = sem("denom_made")
        attn_made = sem("attn_made")
        attn_turned = sem("attn_turned")
        at_hi_made = sem("at_hi_made")
        at_lo_made = sem("at_lo_made")
        o_projected = sem("o_projected")
        res_biased = sem("res_biased")
        x1_made = sem("x1_made")
        n_counted = sem("n_counted")
        n_averaged = sem("n_averaged")
        n_var_made = sem("n_var_made")
        n_rstd_made = sem("n_rstd_made")
        x1_normed = sem("x1_normed")
        x1_kept = sem("x1_kept")
        x1_turned = sem("x1_turned")
        nt_hi_made = sem("nt_hi_made")
        nt_lo_made = sem("nt_lo_made")
        low_summed = sem("low_summed")
        low_hi_made = sem("low_hi_made")
        low_lo_made = sem("low_lo_made")
        up_done = sem("up_done")
        relu_made = sem("relu_made")
        sq_hi_made = sem("sq_hi_made")
        square_made = sem("square_made")
        sq_lo_made = sem("sq_lo_made")
        down_done = sem("down_done")
        y_made = sem("y_made")
        out_made = sem("out_made")
        stored = sem("stored")

        SMALL_LOADS, LOW_LOADS, POOL_CONSTS, STACK_CONSTS = 8, 3, 6, 3
        stack_k_loads = len(K_PARTS) + 1
        stack_q_loads = len(Q_PARTS)
        FV_COL = D + HC

        block = stack.enter_context(nc.Block())

        @block.sync
        def _(sp):
            def x_load(g):
                need(sp, x_turned, 2 * g)
                sp.dma_start(x_in[:, :, :], x[bass.ds(SG * g, SG)].rearrange("b p d -> p b d")).then_inc(x_loaded, 16)
                need(sp, ct_lo_made, g)
                sp.dma_start(c_in[:, :, :], ctx_t[:, bass.ds(TOK * g, TOK)].rearrange("(c p) t -> p c t", p=P)
                             ).then_inc(c_loaded, 16)

            def load(g):
                need(sp, x1_kept, g)
                if isinstance(g, int) and g == 0:
                    sp.wait_ge(w_split, 2)
                sp.dma_start(x1[:, :, :], x[bass.ds(SG * g, SG)].rearrange("b p d -> p b d")).then_inc(res_loaded, 16)

            def shift(g, half):
                cols = slice(half * TOK // 2, (half + 1) * TOK // 2)
                sp.wait_ge(max_rows_made, 2 * g + half + 1)
                sp.dma_start(scratch_max.rearrange("n h t -> (n h) t")[:, cols], max_rows[:, cols]
                             ).then_inc(max_written[half], 16)
                sp.wait_ge(max_written[half], 16 * (g + 1))
                sp.dma_start(q_stack[ROW_MAX:ROW_MAX + 3, :, cols], scratch_max[:, :, cols]
                             ).then_inc(max_loaded[half], 16)

            def x_proj(g, m):
                sp.wait_ge(part_low, 2 * DC * g + m + 1)
                sp.dma_start(scratch_qk[m // DC].rearrange("n (c p) t -> c p n t", p=P)[m % DC],
                             parts[:, m, :, :]).then_inc(parts_written[m], 16)

            def x_stack(g, half):
                cols = slice(half * TOK // 2, (half + 1) * TOK // 2)
                need(sp, s2_done, STEPS * (g - 1) + (half + 1) * STEPS // 2)
                for which, names, tile, done in ((0, Q_PARTS, q_stack, q_stacked), (1, K_PARTS, k_stack, k_stacked)):
                    if half == 0:
                        for c in range(DC):
                            sp.wait_ge(parts_written[DC * which + c], 16 * (g + 1))
                    for n, part in enumerate(names):
                        sp.dma_start(tile[DEPTH * n:DEPTH * (n + 1), :, cols],
                                     scratch_qk[which, part, :, cols].rearrange("(h d) t -> d h t", d=DEPTH)
                                     ).then_inc(done[half], 16)
                row = scratch_mask[bass.ds(g, 1), cols]
                sp.dma_start(k_stack[ROW_MASK:ROW_MASK + 1, :, cols],
                             row.unsqueeze(1).to_broadcast([1, HEADS, TOK // 2])).then_inc(k_stacked[half], 16)

            def store(g):
                sp.wait_ge(out_made, SG * (g + 1))
                sp.dma_start(out[bass.ds(SG * g, SG)].rearrange("b p d -> p b d"), kept[:, :, :]).then_inc(stored, 16)

            def load_weights(half):
                for n in (2 * half, 2 * half + 1):
                    sp.dma_start(w_in[:, n, :, :], (wq, wk, wv, wo)[n].rearrange("(c p) n -> p c n", p=P)
                                 ).then_inc(w_loaded[half], 16)

            def load_ffn(g):
                sp.dma_start(fc_in[:, :, :], w_fc_t.rearrange("(c p) n -> p c n", p=P)).then_inc(fc_loaded, 16)
                sp.dma_start(pj_in[:, :, :], w_proj_t.rearrange("(c p) n -> p c n", p=P)).then_inc(fc_loaded, 16)
                sp.dma_start(v_in[:, :], v).then_inc(low_loaded, 16)
                sp.dma_start(fb_in[:, :], fast_b_t).then_inc(low_loaded, 16)
                sp.dma_start(u_in[:, :], u_t8).then_inc(low_loaded, 16)

            sp.dma_start(x_in[:, :, :], x[0:SG].rearrange("b p d -> p b d")).then_inc(x_loaded, 16)
            load_weights(0)
            for n, b in enumerate((bq, bk)):
                sp.dma_start(bias_qk[:, n, :], b).then_inc(small_loaded, 16)
            for n, s in enumerate((g_xattn, g_ffn, gate)):
                sp.dma_start(gates[:, n:n + 1], s.partition_broadcast(P)).then_inc(small_loaded, 16)
            for tile, b in ((bias_v, bv), (bias_o, bo)):
                sp.dma_start(tile[:, :], b.partition_broadcast(P)).then_inc(small_loaded, 16)
            sp.dma_start(mask_in[:, :], mask.rearrange("(g s) k -> g (s k)", s=SG)).then_inc(small_loaded, 16)
            sp.dma_start(c_in[:, :, :], ctx_t[:, 0:TOK].rearrange("(c p) t -> p c t", p=P)).then_inc(c_loaded, 16)
            load_weights(1)
            sp.wait_ge(mask_made, 1)
            sp.dma_start(scratch_mask, mask_row[:, :]).then_inc(mask_written, 16)
            sp.wait_ge(consts_made, STACK_CONSTS)
            sp.wait_ge(mask_written, 16)

            walk(sp, {"XLoad": x_load, "Load": load, "ShiftTurn": shift, "XParts": x_proj, "XStack": x_stack,
                      "LoadF": load_ffn, "Store": store})
            sp.wait_ge(stored, 16 * GROUPS)

        @block.tensor
        def _(pe):
            def split_product(dst, pairs):
                for n, (lhs, rhs) in enumerate(pairs):
                    mm = pe.matmul(dst, lhs, rhs, start=n == 0, stop=n == len(pairs) - 1)
                return mm

            def prepare(g):
                pe.wait_ge(low_loaded, 16 * LOW_LOADS)
                for c in range(DC):
                    pe.matmul(bank_mix[:, FV_COL + c * RANK:FV_COL + (c + 1) * RANK], v_in[:, c * P:(c + 1) * P],
                                   fb_in[:, :], start=True, stop=True)
                pe.wait_ge(abs_made, 2)
                pe.wait_ge(consts_made, STACK_CONSTS)
                for n in range(2):
                    split_product(bank_f[:, n, :], [(ones[:, :], fc_abs[:, c, n * 512:(n + 1) * 512]) for c in range(DC)])
                split_product(bank_mix[:, 0:D], [(ones[:, :], pj_abs[:, c, :]) for c in range(HC)])
                for u in range(HC):
                    mm = split_product(bank_mix[:, D + u:D + u + 1],
                                       [(fc_abs[:, c, u * P:(u + 1) * P], ones[:, 0:1]) for c in range(DC)])
                mm.then_inc(sums_made, 1)

            def x_turn(g, half):
                pe.wait_ge(x_normed, SG * g + 2 * half + 2)
                if half == 0:
                    need(pe, vals_made, SG * g)
                else:
                    pe.wait_ge(xt_lo_made, 2 * g + 1)
                for c in range(DC):
                    for n in range(2):
                        mm = pe.transpose(bank_x[:, (2 * c + n) * P:(2 * c + n + 1) * P],
                                          x_in[:, 2 * half + n, c * P:(c + 1) * P], ident[:, :])
                mm.then_inc(x_turned, 1)

            def x_proj(g, m):
                which, c = m // DC, m % DC
                hi, lo = (xt_hi, xt_lo) if which == 0 else (ct_hi, ct_lo)
                if m == 0:
                    pe.wait_ge(xt_lo_made, 2 * g + 2)
                    need(pe, w_split, 1)
                else:
                    pe.wait_ge(qk_biased, 2 * DC * g + m)
                if m == DC:
                    pe.wait_ge(ct_hi_made, g + 1)
                    pe.wait_ge(ct_lo_made, g + 1)
                cols = slice(c * P, (c + 1) * P)
                split_product(bank_x[:, :], [(w[:, which, k, cols], t[:, k, :])
                                             for w, t in ((w_hi, hi), (w_lo, hi), (w_hi, lo)) for k in range(DC)]
                              ).then_inc(qk_projected, 1)

            def x_val(g, b):
                if b == 0:
                    pe.wait_ge(qk_biased, 2 * DC * (g + 1))
                    need(pe, w_split, 2)
                else:
                    pe.wait_ge(vals_made, SG * g + b)
                toks = slice(b * SEQ, (b + 1) * SEQ)
                split_product(bank_x[:, 0:D], [(t[:, k, toks], w[:, 2, k, :])
                                               for w, t in ((w_hi, ct_hi), (w_lo, ct_hi), (w_hi, ct_lo)) for k in range(DC)]
                              ).then_inc(v_projected, 1)

            def max_scores(g, s):
                b, quarter = s // QUARTERS, s % QUARTERS
                if s % (STEPS // 2) == 0:
                    half = 2 * s // STEPS
                    pe.wait_ge(q_stacked[half], 16 * stack_q_loads * (g + 1))
                    pe.wait_ge(k_stacked[half], 16 * stack_k_loads * (g + 1))
                if s < 2:
                    need(pe, exp_done, STEPS * g - 1 + s)
                else:
                    pe.wait_ge(max_taken, STEPS * g + s - 1)
                toks = slice(b * SEQ, (b + 1) * SEQ)
                for n in range(4):
                    h = 4 * quarter + n
                    mm = pe.matmul(bank_score[:, s % 2, n * SEQ:(n + 1) * SEQ], q_stack[0:ROWS_S1, h, toks],
                                   k_stack[0:ROWS_S1, h, toks], start=True, stop=True)
                mm.then_inc(s1_done, 1)

            def shift(g, half):
                pe.wait_ge(max_split, 2 * g + half + 1)
                if half == 0:
                    need(pe, nt_lo_made, 2 * g)
                else:
                    pe.wait_ge(max_rows_made, 2 * g + 1)
                rows = bank_t[0:MAX_SLOTS * HEADS, 0, 0:TOK // 2].bitcast(BF16)
                for b in range(2 * half, 2 * half + 2):
                    mm = pe.transpose(rows[:, b * SEQ:(b + 1) * SEQ],
                                      max_parts[:, b, :, :].rearrange("p n h -> p (n h)"), ident16[:, :])
                mm.then_inc(max_turned, 1)

            def exp_scores(g, s):
                b, quarter = s // QUARTERS, s % QUARTERS
                if s % (STEPS // 2) == 0:
                    pe.wait_ge(max_loaded[2 * s // STEPS], 16 * (g + 1))
                if s < 2:
                    pe.wait_ge(max_taken, STEPS * g + STEPS - 1 + s)
                else:
                    pe.wait_ge(exp_done, STEPS * g + s - 1)
                toks = slice(b * SEQ, (b + 1) * SEQ)
                for n in range(4):
                    h = 4 * quarter + n
                    mm = pe.matmul(bank_score[:, s % 2, n * SEQ:(n + 1) * SEQ], k_stack[0:ROWS_S2, h, toks],
                                   q_stack[0:ROWS_S2, h, toks], start=True, stop=True)
                mm.then_inc(s2_done, 1)

            def mix(g, s):
                b, quarter = s // QUARTERS, s % QUARTERS
                pe.wait_ge(exp_done, STEPS * g + s + 1)
                if quarter == 0:
                    pe.wait_ge(vals_made, SG * g + b + 1)
                    need(pe, mix_evicted, SG * g + b)
                    if isinstance(g, int) and g == 0:
                        pe.wait_ge(sums_read, 2)
                for n in range(4):
                    mm = pe.matmul(bank_mix[STRIP * n:STRIP * (n + 1), quarter * SEQ:(quarter + 1) * SEQ],
                                   vals[:, b, 4 * quarter + n, :], probs[:, s % PROB_BUFFERS, n, :], start=True, stop=True)
                mm.then_inc(mix_done, 1)

            def turn4(g, b):
                pe.wait_ge(mix_evicted, SG * g + b + 1)
                if b == 0:
                    pe.wait_ge(max_rows_made, 2 * g + 2)
                else:
                    pe.wait_ge(x1_made, SG * g + b)
                for n in range(QUARTERS):
                    mm = pe.transpose(bank_t[:, 0, n * P:(n + 1) * P], mix_t[:, n * P:(n + 1) * P], ident[:, :])
                mm.then_inc(mix_turned, 1)

            def turn2(g, b):
                pe.wait_ge(attn_made, SG * g + b + 1)
                if b == 0:
                    need(pe, nt_lo_made, 2 * g)
                else:
                    pe.wait_ge(at_lo_made, SG * g + b)
                for c in range(DC):
                    mm = pe.transpose(bank_t[:, 1, c * P:(c + 1) * P], attn[:, c * P:(c + 1) * P], ident[:, :])
                mm.then_inc(attn_turned, 1)

            def out_proj(g, b):
                pe.wait_ge(at_lo_made, SG * g + b + 1)
                split_product(bank_t[:, 0, 0:D], [(t[:, k, :], w[:, 3, k, :])
                                                  for w, t in ((w_hi, at_hi), (w_lo, at_hi), (w_hi, at_lo)) for k in range(DC)]
                              ).then_inc(o_projected, 1)

            def turn3(g, pair):
                pe.wait_ge(x1_normed, SG * g + 2 * pair + 2)
                pe.wait_ge(at_lo_made, SG * (g + 1))
                for c in range(DC):
                    for n in range(2):
                        mm = pe.transpose(bank_t[:, 1 - pair, (2 * c + n) * P:(2 * c + n + 1) * P],
                                          x1_norm[:, 2 * pair + n, c * P:(c + 1) * P], ident[:, :])
                mm.then_inc(x1_turned, 1)

            def low_rank(g):
                pe.wait_ge(nt_lo_made, 2 * (g + 1))
                need(pe, low_made, 2)
                split_product(bank_f[:, 0, :], [(fv_rows[:, k, :, :].rearrange("p a r -> p (a r)"), t[:, k, :])
                                                for t in (nt_hi, nt_lo) for k in range(DC)]).then_inc(low_summed, 1)

            def up(g, u):
                cols = slice(u * P, (u + 1) * P)
                if u == 1:
                    pe.wait_ge(low_lo_made, g + 1)
                elif u > 1:
                    pe.wait_ge(relu_made, HC * g + u - 1)
                dst = bank_f[:, (u + 1) % 2, :]
                if u == 0:
                    need(pe, tern_made, 2)
                for n, (t, k) in enumerate((t, k) for t in (nt_hi, nt_lo) for k in range(DC)):
                    pe.matmul(dst, fc_tern[:, k, cols], t[:, k, :], start=n == 0, stop=False)
                if u == 0:
                    pe.wait_ge(low_lo_made, g + 1)
                pe.matmul(dst, u_rows[:, cols], low_rows[:, :], start=False, stop=True).then_inc(up_done, 1)

            def down(g, n):
                b, half = n // 2, n % 2
                toks = slice(b * SEQ, (b + 1) * SEQ)
                dst = bank_f[:, (b + 1) % 2, 0:D]
                if n == 0:
                    pe.wait_ge(relu_made, HC * g + HC - 1)
                elif n == 2:
                    pe.wait_ge(relu_made, HC * g + HC)
                elif half == 0:
                    pe.wait_ge(y_made, SG * g + b - 1)
                for u in range(half * HC // 2, (half + 1) * HC // 2):
                    if b == 0:
                        pe.wait_ge(sq_lo_made, HC * g + u + 1)
                        pe.wait_ge(sq_hi_made, HC * g + u + 1)
                    pe.matmul(dst, sq_hi[:, u, toks], pj_tern[:, u, :], start=u == 0, stop=False)
                    mm = pe.matmul(dst, sq_lo[:, u, toks], pj_tern[:, u, :], start=False, stop=u == HC - 1)
                if half == 1:
                    mm.then_inc(down_done, 1)

            pe.wait_ge(pool_consts, POOL_CONSTS)
            walk(pe, {"Prepare": prepare, "XTurn": x_turn, "XProj": x_proj, "XVal": x_val, "Max": max_scores, "ShiftTurn": shift,
                      "Exp": exp_scores, "Mix": mix, "Turn4": turn4, "Turn2": turn2, "Out": out_proj,
                      "Turn3": turn3, "LowRank": low_rank, "Up": up, "Down": down})

        @block.scalar
        def _(act):
            def weights(g, half):
                pair = slice(2 * half, 2 * half + 2)
                act.wait_ge(w_loaded[half], 32)
                if half == 1:
                    act.wait_ge(wo_gated, 1)
                act.activation(w_hi[:, pair, :, :], w_in[:, pair, :, :], ACT.Copy).then_inc(w_high, 1)
                if half == 0:
                    act.wait_ge(small_loaded, 16 * SMALL_LOADS)
                    act.activation(gates[:, 0:2], gates[:, 0:2], ACT.Tanh).then_inc(gates_made, 1)

            def prepare(g):
                act.wait_ge(fc_loaded, 32)
                for w, w_abs in ((fc_in, fc_abs), (pj_in, pj_abs)):
                    act.activation(w_abs[:, :, :], w[:, :, :], ACT.Abs).then_inc(abs_made, 1)
                act.wait_ge(abs_made, 2)
                for w in (fc_in, pj_in):
                    act.activation(w[:, :, :], w[:, :, :], ACT.Sign).then_inc(signs_made, 1)

            def x_turn(g, half):
                act.wait_ge(x_turned, 2 * g + half + 1)
                need(act, qk_projected, 2 * DC * g)
                act.activation(xt_hi[:, :, 2 * half * SEQ:2 * (half + 1) * SEQ],
                               bank_x[:, :].rearrange("p (c t) -> p c t", c=DC), ACT.Copy).then_inc(xt_hi_made, 1)

            def x_ctx(g):
                act.wait_ge(c_loaded, 16 * (g + 1))
                need(act, v_projected, SG * g)
                act.activation(ct_hi[:, :, :], c_in[:, :, :], ACT.Copy).then_inc(ct_hi_made, 1)

            def x_proj(g, m):
                act.wait_ge(qk_projected, 2 * DC * g + m + 1)
                need(act, part_rest, 2 * DC * g + m - 1)
                act.activation(qk[:, m % 2, :], bank_x[:, :], ACT.Identity,
                               bias=bias_qk[:, m // DC, m % DC:m % DC + 1]).then_inc(qk_biased, 1)

            def shift(g, half):
                cols = slice(half * TOK // 2, (half + 1) * TOK // 2)
                act.wait_ge(max_turned, 2 * g + half + 1)
                need(act, max_written[half], 16 * g)
                act.activation(max_rows[:, cols], bank_t[0:3 * HEADS, 0, 0:TOK // 2].bitcast(BF16)[:, cols], ACT.Copy
                               ).then_inc(max_rows_made, 1)

            def exp_scores(g, s):
                act.wait_ge(s2_done, STEPS * g + s + 1)
                need(act, mix_done, STEPS * g + max(0, s + 1 - PROB_BUFFERS))
                act.activation(probs[:, s % PROB_BUFFERS, :, :].rearrange("p n t -> p (n t)"), bank_score[:, s % 2, :], ACT.Exp,
                               scale=float(DEPTH) ** -0.5).then_inc(exp_done, 1)

            def turn2(g, b):
                act.wait_ge(attn_turned, SG * g + b + 1)
                need(act, o_projected, SG * g + b)
                act.activation(at_hi[:, :, :], bank_t[:, 1, 0:D].rearrange("p (c t) -> p c t", c=DC), ACT.Copy
                               ).then_inc(at_hi_made, 1)

            def keep(g):
                act.wait_ge(x1_normed, SG * (g + 1))
                need(act, stored, 16 * g)
                act.activation(kept[:, :, :], x1[:, :, :], ACT.Copy).then_inc(x1_kept, 1)
                if isinstance(g, int) and g == 0:
                    act.wait_ge(low_made, 2)

            def turn3(g, pair):
                act.wait_ge(x1_turned, 2 * g + pair + 1)
                act.activation(nt_hi[:, :, 2 * pair * SEQ:2 * (pair + 1) * SEQ],
                               bank_t[:, 1 - pair, :].rearrange("p (c t) -> p c t", c=DC), ACT.Copy
                               ).then_inc(nt_hi_made, 1)

            def low_rank(g):
                act.wait_ge(low_summed, g + 1)
                act.activation(low_rows[:, :], bank_f[:, 0, :], ACT.Copy).then_inc(low_hi_made, 1)

            def up(g, u):
                act.wait_ge(up_done, HC * g + u + 1)
                if u >= 2:
                    act.wait_ge(square_made, HC * g + u - 1)
                act.activation(relu[:, u % 2, :], bank_f[:, (u + 1) % 2, :], ACT.Relu, scale=fc_scale[:, u:u + 1]
                               ).then_inc(relu_made, 1)
                act.wait_ge(relu_made, HC * g + u + 1)
                act.activation(sq_hi[:, u, :], relu[:, u % 2, :], ACT.Square).then_inc(sq_hi_made, 1)

            walk(act, {"Weights": weights, "Prepare": prepare, "XTurn": x_turn, "XCtx": x_ctx, "XProj": x_proj, "ShiftTurn": shift, "Exp": exp_scores, "Turn2": turn2,
                       "Keep": keep, "Turn3": turn3, "LowRank": low_rank, "Up": up})

        @block.vector
        def _(dve):
            def weights(g, half):
                pair = slice(2 * half, 2 * half + 2)
                if half == 0:
                    dve.wait_ge(small_loaded, 16 * SMALL_LOADS)
                    dve.tensor_scalar(mask_row[:, :], mask_in[:, :], MASKED, MASKED, ALU.mult, ALU.subtract
                                      ).then_inc(mask_made, 1)
                else:
                    dve.wait_ge(w_loaded[1], 32)
                    dve.wait_ge(gates_made, 1)
                    dve.tensor_scalar(w_in[:, 3, :, :], w_in[:, 3, :, :], gates[:, 0:1], None, ALU.mult).then_inc(wo_gated, 1)
                    dve.tensor_scalar(bias_o[:, :], bias_o[:, :], gates[:, 0:1], None, ALU.mult).then_inc(gates_made, 1)
                dve.wait_ge(w_high, half + 1)
                dve.tensor_tensor(w_lo[:, pair, :, :], w_in[:, pair, :, :], w_hi[:, pair, :, :].bitcast(F32), ALU.subtract
                                  ).then_inc(w_split, 1)

            def prepare(g):
                dve.wait_ge(sums_made, 1)
                dve.tensor_scalar(scale_row[:, :], bank_f[:, :, :].rearrange("p a n -> p (a n)"), 1.0 / D, SCALE_MIN,
                                  ALU.mult, ALU.max).then_inc(scales_made, 1)
                dve.tensor_scalar(fc_scale[:, :], bank_mix[:, D:D + HC], 1.0 / D, SCALE_MIN, ALU.mult, ALU.max
                                  ).then_inc(scales_made, 1)
                dve.tensor_scalar(pj_scale[:, :], bank_mix[:, 0:D], 1.0 / HID, SCALE_MIN, ALU.mult, ALU.max
                                  ).then_inc(sums_read, 1)
                dve.wait_ge(scales_made, 2)
                dve.wait_ge(sums_read, 1)
                dve.tensor_scalar(half_scale[:, 0, :], scale_row[:, :], 0.5, None, ALU.mult).then_inc(scales_made, 1)
                dve.tensor_scalar(pj_half[:, :], pj_scale[:, :], 0.5, None, ALU.mult).then_inc(scales_made, 1)
                dve.tensor_scalar(pj_gain[:, :], pj_scale[:, :], gates[:, 1:2], None, ALU.mult).then_inc(scales_made, 1)
                dve.tensor_copy(fv[:, :, :], bank_mix[:, FV_COL:FV_COL + DC * RANK].rearrange("p (c r) -> p c r", c=DC)
                                ).then_inc(sums_read, 1)
                dve.wait_ge(scales_made, 5)
                for c in range(DC):
                    last = dve.tensor_tensor(fc_abs[:, c, :], fc_abs[:, c, :], half_scale[:, 0, :], ALU.is_gt)
                last.then_inc(over_half, 1)
                last = dve.tensor_tensor(pj_abs[:, :, :], pj_abs[:, :, :],
                                         pj_half[:, :].unsqueeze(1).to_broadcast([P, HC, D]), ALU.is_gt)
                last.then_inc(over_half, 1)
                dve.reciprocal(half_scale[:, 1, :], scale_row[:, :]).then_inc(scales_made, 1)
                dve.tensor_scalar(u_in[:, :], u_in[:, :], gates[:, 2:3], None, ALU.mult).then_inc(scales_made, 1)
                dve.wait_ge(sums_read, 2)
                dve.tensor_copy(fv_hi[:, :, :], fv[:, :, :]).then_inc(scales_made, 1)
                dve.wait_ge(scales_made, 8)
                dve.tensor_tensor(u_in[:, :], u_in[:, :], half_scale[:, 1, :], ALU.mult).then_inc(scales_made, 1)
                for a in range(0, P // RANK, 2):
                    dve.tensor_copy(fv_rows[:, :, a, :], fv_hi[:, :, :].bitcast(F32))
                    dve.tensor_tensor(fv_rows[:, :, a + 1, :], fv[:, :, :], fv_hi[:, :, :].bitcast(F32), ALU.subtract)
                dve.wait_ge(scales_made, 9)
                dve.tensor_copy(u_rows[:, :], u_in[:, :]).then_inc(low_made, 1)
                dve.wait_ge(low_made, 1)
                for q in (1, 3):
                    rows = slice(32 * q, 32 * (q + 1))
                    last = dve.tensor_tensor(u_rows[rows, :], u_in[rows, :], u_rows[rows, :].bitcast(F32), ALU.subtract)
                last.then_inc(low_made, 1)

            def x_stats(g):
                dve.wait_ge(x_loaded, 16 * (g + 1))
                need(dve, x_rstd_made, g)
                for b in range(SG):
                    last = dve.bn_stats(x_stat[:, b, :], x_in[:, b, :])
                last.then_inc(x_counted, 1)
                dve.wait_ge(x_counted, g + 1)
                dve.memset(hold[:, :], 0.0)
                for b in range(SG):
                    last = dve.bn_aggr(x_mean[:, b, :], x_stat[:, b, :])
                last.then_inc(x_averaged, 1)

            def x_normalise(g):
                dve.wait_ge(x_rstd_made, g + 1)
                for b in range(SG):
                    dve.tensor_scalar(x_in[:, b, :], x_in[:, b, :], x_mean[:, b, 0:1], x_rstd[:, b:b + 1],
                                      ALU.subtract, ALU.mult).then_inc(x_normed, 1)

            def x_turn(g, half):
                dve.wait_ge(xt_hi_made, 2 * g + half + 1)
                cols = slice(2 * half * SEQ, 2 * (half + 1) * SEQ)
                dve.tensor_tensor(xt_lo[:, :, cols], bank_x[:, :].rearrange("p (c t) -> p c t", c=DC),
                                  xt_hi[:, :, cols].bitcast(F32), ALU.subtract).then_inc(xt_lo_made, 1)

            def x_proj(g, m):
                dve.wait_ge(qk_biased, 2 * DC * g + m + 1)
                need(dve, parts_written[m], 16 * g)
                dve.tensor_copy(parts[:, m, 0, :], qk[:, m % 2, :]).then_inc(part_high, 1)

            def x_val(g, b):
                dve.wait_ge(v_projected, SG * g + b + 1)
                if isinstance(g, int) and g == 0:
                    dve.wait_ge(pool_consts, POOL_CONSTS)
                else:
                    need(dve, mix_done, STEPS * (g - 1) + QUARTERS * (b + 1))
                dve.tensor_tensor(vals[:, b, :, 0:DEPTH], bank_x[:, 0:D].rearrange("p (h d) -> p h d", h=HEADS),
                                  bias_v[:, :].rearrange("p (h d) -> p h d", h=HEADS), ALU.add).then_inc(vals_made, 1)

            def take_max(g, s):
                b, quarter = s // QUARTERS, s % QUARTERS
                dve.wait_ge(s1_done, STEPS * g + s + 1)
                dve.tensor_reduce(maxima[:, b, 4 * quarter:4 * quarter + 4],
                                  bank_score[:, s % 2, :].rearrange("p (n k) -> p n k", n=4), AX_X, ALU.max
                                  ).then_inc(max_taken, 1)

            def shift(g, half):
                bs = slice(2 * half, 2 * half + 2)
                done = 2 * g + half + 1
                dve.wait_ge(max_taken, STEPS * g + (half + 1) * STEPS // 2)
                need(dve, max_turned, 2 * g)
                dve.tensor_scalar(max_parts[:, bs, 0, :], maxima[:, bs, :], -1.0, None, ALU.mult).then_inc(max_high, 1)
                dve.wait_ge(max_high, done)
                dve.scalar_tensor_tensor(max_rest[:, bs, :], maxima[:, bs, :], -1.0, max_parts[:, bs, 0, :], ALU.mult,
                                         ALU.subtract).then_inc(max_rest_made, 1)
                dve.wait_ge(max_rest_made, done)
                dve.tensor_copy(max_parts[:, bs, 1, :], max_rest[:, bs, :]).then_inc(max_mid, 1)
                dve.wait_ge(max_mid, done)
                dve.tensor_tensor(max_parts[:, bs, 2, :], max_rest[:, bs, :], max_parts[:, bs, 1, :], ALU.subtract
                                  ).then_inc(max_split, 1)

            def evict(g, b):
                dve.wait_ge(mix_done, STEPS * g + QUARTERS * (b + 1))
                need(dve, mix_turned, SG * g + b)
                dve.tensor_copy(mix_t[:, :], bank_mix[:, :]).then_inc(mix_evicted, 1)

            def turn4(g, b):
                heads = bank_t[:, 0, :].rearrange("p (h e) -> p h e", h=HEADS)
                dve.wait_ge(mix_turned, SG * g + b + 1)
                dve.reciprocal(denom[:, :], heads[:, :, DEPTH]).then_inc(denom_made, 1)
                dve.wait_ge(denom_made, SG * g + b + 1)
                need(dve, attn_turned, SG * g + b)
                dve.tensor_tensor(attn[:, :].rearrange("p (h d) -> p h d", h=HEADS), heads[:, :, 0:DEPTH],
                                  denom[:, :].unsqueeze(2).to_broadcast([P, HEADS, DEPTH]), ALU.mult).then_inc(attn_made, 1)

            def turn2(g, b):
                dve.wait_ge(at_hi_made, SG * g + b + 1)
                dve.tensor_tensor(at_lo[:, :, :], bank_t[:, 1, 0:D].rearrange("p (c t) -> p c t", c=DC),
                                  at_hi[:, :, :].bitcast(F32), ALU.subtract).then_inc(at_lo_made, 1)

            def out_proj(g, b):
                dve.wait_ge(o_projected, SG * g + b + 1)
                dve.wait_ge(res_biased, g + 1)
                dve.tensor_tensor(x1[:, b, :], bank_t[:, 0, 0:D], x1[:, b, :], ALU.add).then_inc(x1_made, 1)
                dve.wait_ge(x1_made, SG * g + b + 1)
                need(dve, n_averaged, g)
                dve.bn_stats(n_stat[:, b, :], x1[:, b, :]).then_inc(n_counted, 1)

            def stats2(g):
                dve.wait_ge(n_counted, SG * (g + 1))
                dve.memset(hold[:, :], 0.0)
                for b in range(SG):
                    last = dve.bn_aggr(n_mean[:, b, :], n_stat[:, b, :])
                last.then_inc(n_averaged, 1)

            def norm2(g):
                dve.wait_ge(n_rstd_made, g + 1)
                need(dve, x1_turned, 2 * g)
                for b in range(SG):
                    dve.tensor_scalar(x1_norm[:, b, :], x1[:, b, :], n_mean[:, b, 0:1], n_rstd[:, b:b + 1],
                                      ALU.subtract, ALU.mult).then_inc(x1_normed, 1)

            def turn3(g, pair):
                dve.wait_ge(nt_hi_made, 2 * g + pair + 1)
                toks = slice(2 * pair * SEQ, 2 * (pair + 1) * SEQ)
                dve.tensor_tensor(nt_lo[:, :, toks], bank_t[:, 1 - pair, :].rearrange("p (c t) -> p c t", c=DC),
                                  nt_hi[:, :, toks].bitcast(F32), ALU.subtract).then_inc(nt_lo_made, 1)

            def low_rank(g):
                dve.wait_ge(low_hi_made, g + 1)
                dve.tensor_tensor(low_rows[64:P, :], bank_f[64:P, 0, :], low_rows[64:P, :].bitcast(F32), ALU.subtract
                                  ).then_inc(low_lo_made, 1)

            def up(g, u):
                dve.wait_ge(square_made, HC * g + u + 1)
                dve.wait_ge(sq_hi_made, HC * g + u + 1)
                dve.tensor_tensor(sq_lo[:, u, :], square[:, u % 2, :], sq_hi[:, u, :].bitcast(F32), ALU.subtract
                                  ).then_inc(sq_lo_made, 1)

            def down(g, b):
                dve.wait_ge(down_done, SG * g + b + 1)
                if b >= 2:
                    dve.wait_ge(out_made, SG * g + b - 1)
                dve.tensor_tensor(y[:, b % 2, :], bank_f[:, (b + 1) % 2, 0:D], pj_gain[:, :], ALU.mult).then_inc(y_made, 1)

            dve.memset(max_parts[:, :, :, :], 0.0)
            dve.memset(ones[:, :], 1.0).then_inc(consts_made, 1)
            dve.memset(q_stack[ROWS_QK:P, :, :], 1.0).then_inc(consts_made, 1)
            dve.memset(k_stack[ROWS_QK:P, :, :], 1.0).then_inc(consts_made, 1)
            walk(dve, {"Weights": weights, "Prepare": prepare, "XStats": x_stats, "XNorm": x_normalise, "XTurnLow": x_turn,
                       "XParts": x_proj, "XValSum": x_val, "Max": take_max, "Shift": shift, "Evict": evict, "Norm4": turn4,
                       "Turn2Low": turn2, "OutSum": out_proj, "Stats2": stats2, "Norm2": norm2, "Turn3Low": turn3,
                       "LowRankLow": low_rank, "UpLow": up, "Gain": down})

        @block.gpsimd
        def _(pool):
            def prepare(g):
                for n, (tern, w_sign, over) in enumerate(((fc_tern, fc_in, fc_abs), (pj_tern, pj_in, pj_abs))):
                    pool.wait_ge(signs_made, n + 1)
                    pool.wait_ge(over_half, n + 1)
                    pool.tensor_tensor(tern[:, :, :], w_sign[:, :, :], over[:, :, :], ALU.mult).then_inc(tern_made, 1)

            def x_stats(g):
                pool.wait_ge(x_averaged, g + 1)
                pool.tensor_tensor(x_var[:, :], x_mean[:, :, 1], eps[:, :], ALU.add).then_inc(x_var_made, 1)
                pool.wait_ge(x_var_made, g + 1)
                need(pool, x_normed, SG * g)
                pool.tensor_tensor(x_rstd[:, :], x_var[:, :], power[:, :], ALU.pow).then_inc(x_rstd_made, 1)

            def x_ctx(g):
                pool.wait_ge(ct_hi_made, g + 1)
                pool.tensor_tensor(ct_lo[:, :, :], c_in[:, :, :], ct_hi[:, :, :].bitcast(F32), ALU.subtract
                                   ).then_inc(ct_lo_made, 1)

            def x_proj(g, m):
                pool.wait_ge(part_high, 2 * DC * g + m + 1)
                pool.tensor_tensor(parts[:, m, 1, :], qk[:, m % 2, :], parts[:, m, 0, :], ALU.subtract)
                need(pool, part_low, 2 * DC * g + m)
                pool.tensor_tensor(rest[:, :], qk[:, m % 2, :], parts[:, m, 0, :], ALU.subtract).then_inc(part_rest, 1)
                pool.wait_ge(part_rest, 2 * DC * g + m + 1)
                pool.tensor_tensor(parts[:, m, 2, :], rest[:, :], parts[:, m, 1, :], ALU.subtract
                                   ).then_inc(part_low, 1)

            def bias(g):
                pool.wait_ge(res_loaded, 16 * (g + 1))
                if isinstance(g, int) and g == 0:
                    pool.wait_ge(gates_made, 2)
                for b in range(SG):
                    last = pool.tensor_tensor(x1[:, b, :], x1[:, b, :], bias_o[:, :], ALU.add)
                last.then_inc(res_biased, 1)

            def stats2(g):
                pool.wait_ge(n_averaged, g + 1)
                pool.tensor_tensor(n_var[:, :], n_mean[:, :, 1], eps[:, :], ALU.add).then_inc(n_var_made, 1)
                pool.wait_ge(n_var_made, g + 1)
                need(pool, x1_normed, SG * g)
                pool.tensor_tensor(n_rstd[:, :], n_var[:, :], power[:, :], ALU.pow).then_inc(n_rstd_made, 1)

            def up(g, u):
                pool.wait_ge(relu_made, HC * g + u + 1)
                if u >= 2:
                    pool.wait_ge(sq_lo_made, HC * g + u - 1)
                pool.tensor_tensor(square[:, u % 2, :], relu[:, u % 2, :], relu[:, u % 2, :], ALU.mult
                                   ).then_inc(square_made, 1)

            def down(g, b):
                pool.wait_ge(y_made, SG * g + b + 1)
                pool.tensor_tensor(kept[:, b, :], y[:, b % 2, :], kept[:, b, :], ALU.add).then_inc(out_made, 1)

            pool.memset(power[:, :], -0.5)
            pool.memset(eps[:, :], EPS).then_inc(pool_consts, 1)
            pool.memset(ident[:, :], 0.0).then_inc(pool_consts, 1)
            pool.memset(ident16[:, :], 0.0).then_inc(pool_consts, 1)
            pool.wait_ge(pool_consts, 3)
            for tile in (ident, ident16):
                pool.affine_select(out=tile[:, :], in_=tile[:, :], compare_op=ALU.not_equal, fill=1.0, base=0,
                                   pattern=[[-1, P]], channel_multiplier=1).then_inc(pool_consts, 1)
            pool.memset(vals[:, :, :, :], 1.0).then_inc(pool_consts, 1)
            walk(pool, {"XStats": x_stats, "XCtx": x_ctx, "XParts": x_proj, "Bias": bias, "Stats2": stats2,
                        "Prepare": prepare, "Up": up, "Gain": down})


def kernel(**inputs):
    import numpy as np
    import concourse.bacc as bacc
    from concourse.bass_utils import run_bass_kernel_spmd

    def laid_out(a):
        return np.ascontiguousarray(a)

    take = {name: np.asarray(a) for name, a in inputs.items()}
    arrays = {
        "x": take["x"],
        "ctx_t": take["ctx_1024"].reshape(SEQS * SEQ, D).T,
        "mask": take["mask_BxS2_bk1"],
        "g_xattn": take["g_xattn"],
        "g_ffn": take["g_ffn"],
        "wq": take["L0_xattn_Wq"], "bq": take["L0_xattn_bq"].reshape(DC, P).T,
        "wk": take["L0_xattn_Wk"], "bk": take["L0_xattn_bk"].reshape(DC, P).T,
        "wv": take["L0_xattn_Wv"], "bv": take["L0_xattn_bv"],
        "wo": take["L0_xattn_Wo"], "bo": take["L0_xattn_bo"],
        "fast_b_t": take["L0_ffn_fast_b"].T,
        "w_fc_t": take["L0_ffn_w_fc"].T,
        "w_proj_t": take["L0_ffn_w_proj"].T,
        "u_t8": np.tile(take["L0_ffn_u"].T, (P // RANK, 1)),
        "v": take["L0_ffn_v"],
        "gate": take["L0_ffn_gate"].reshape(1),
    }
    nc = bacc.Bacc("TRN2", target_bir_lowering=False, num_devices=1)
    feed, args = {}, {}
    for name, a in arrays.items():
        a = laid_out(a)
        feed[f"in_{name}"] = a
        args[name] = nc.dram_tensor(f"in_{name}", a.shape, mybir.dt.from_np(a.dtype), kind="ExternalInput").ap()
    args["out"] = nc.dram_tensor("out_x", (SEQS, SEQ, D), F32, kind="ExternalOutput").ap()
    build_block(nc, **args)
    result = run_bass_kernel_spmd(nc, [feed], core_ids=[0])
    return result.results[0]["out_x"]
```

```python
from contextlib import ExitStack

import concourse.bass as bass
from concourse import mybir

F32 = mybir.dt.float32
F32R = mybir.dt.float32r
BF16 = mybir.dt.bfloat16
ALU = mybir.AluOpType
ACT = mybir.ActivationFunctionType
AX_X = mybir.AxisListType.X

P = 128
SEQS, SEQ, D = 32, 128, 256
HEADS = 16
DEPTH = D // HEADS
HID = 1024
RANK = 16
SG = 4
GROUPS = SEQS // SG
TOK = SG * SEQ
DC = D // P
HC = HID // P
QUARTERS = HEADS // 4
STEPS = SG * QUARTERS
STRIP = 32
PROB_BUFFERS = 3
MIX_LAG = 2
LAST_TAIL = (("Turn4", 0), ("Norm4", 0), ("Turn2", 1), ("Turn2Low", 2), ("Out", 3), ("OutSum", 3))
STATS2_AT, NORM2_AT, TURN3_AT, LOW_RANK_AT = 3, 5, (6, 7), 8
X_CTX_AT, X_TURN_AT, X_LOAD_AT, LOAD_AT = 7, (2, 5), 8, 7
UP_AT = (10, 11, 13, 14, 16, 17, 19, 20)
UP_LAG = 2
X_PROJ_AT = (8, 12, 15, 18)
BIAS_AT = 22
X_VAL_AT = (24, 28)
DOWN_AT = (21, 23, 25, 26, 27, 29, 31, 33)
STACK0_AT, X_STATS_AT, X_NORM_AT = 26, 24, 28
TAIL_LAGS = (("Turn4", 1), ("Norm4", 1), ("Turn2", 2), ("Turn2Low", 3), ("Out", 4), ("OutSum", 4))
SLOTS = 2 * STEPS + MIX_LAG
MAX_SLOTS = 5
EPS = 1e-5
SCALE_MIN = 1e-5
MASKED = 1e30
TWO_ONES = 1 + 2.0 ** -9 - 2.0 ** -16

K_PARTS = [0, 0, 1, 1, 0, 2]
Q_PARTS = [0, 1, 0, 1, 2, 0]
ROWS_QK = DEPTH * len(K_PARTS)
ROW_MASK = ROWS_QK
ROW_MAX = ROWS_QK + 1
ROWS_S1 = ROWS_QK + 1
ROWS_S2 = ROWS_QK + 4


def schedule(before, after):
    at = [[] for _ in range(SLOTS)]

    def put(slot, distance, name, *arg):
        if -before <= distance <= after:
            at[min(slot, SLOTS - 1)].append((distance, name, *arg))

    for half, slot in enumerate(X_TURN_AT):
        put(slot, 1, "XTurn", half)
        put(slot + 1, 1, "XTurnLow", half)
    put(STEPS + STEPS + MIX_LAG - 1, 0, "Evict", SG - 1)
    for b in range(SG - 1):
        put(STEPS + QUARTERS * (b + 1) + MIX_LAG - 1, 0, "Evict", b)
    for b in range(SG - 1):
        for name, lag in TAIL_LAGS:
            put(STEPS + QUARTERS * (b + 1) + MIX_LAG - 1 + lag, 0, name, b)
    for name, slot in LAST_TAIL:
        put(slot, -1, name, SG - 1)
    put(LOAD_AT, 0, "Load")
    put(BIAS_AT, 0, "Bias")
    for m, slot in enumerate(X_PROJ_AT):
        put(slot, 1, "XProj", m)
        for n, name in enumerate(("XHigh", "XMid", "XLow")):
            put(slot + 1 + (n > 0), 1, name, m)
    put(STATS2_AT, -1, "Stats2")
    put(NORM2_AT, -1, "Norm2")
    put(NORM2_AT, -1, "Keep")
    for half, slot in enumerate(TURN3_AT):
        put(slot, -1, "Turn3", half)
        put(slot + 1, -1, "Turn3Low", half)
    put(STEPS // 2, 0, "Shift", 0)
    put(STEPS // 2 + 1, 0, "ShiftTurn", 0)
    put(STEPS - 1, 0, "Shift", 1)
    put(STEPS + 1, 0, "ShiftTurn", 1)
    put(LOW_RANK_AT, -1, "LowRank")
    put(LOW_RANK_AT + 1, -1, "LowRankLow")
    for u, slot in enumerate(UP_AT):
        put(slot, -1, "Up", u)
        put(slot + UP_LAG, -1, "UpLow", u)
    for n, slot in enumerate(DOWN_AT):
        put(slot, -1, "Down", n)
        if n % 2 == 1:
            put(slot + 1, -1, "Gain", n // 2)
    for b in range(len(X_VAL_AT), SG):
        put(b - len(X_VAL_AT), 0, "XVal", b)
        put(b - len(X_VAL_AT), 0, "XValSum", b)
    put(X_CTX_AT, 1, "XCtx")
    put(X_LOAD_AT, 2, "XLoad")
    for b, slot in enumerate(X_VAL_AT):
        put(slot, 1, "XVal", b)
        put(slot + 1, 1, "XValSum", b)
    put(X_STATS_AT, 2, "XStats")
    put(X_NORM_AT, 2, "XNorm")
    put(STACK0_AT, 1, "XStack", 0)
    put(2 * STEPS, 1, "XStack", 1)
    put(SLOTS - 1, -1, "Store")
    if not before:
        for n, slot in enumerate((1, 30)):
            put(slot, 0, "Ternary", n)
        for n, slot in enumerate((27, 29)):
            put(slot, 0, "OverHalf", 2 + n)
        for n, slot in enumerate((20, 22, 25)):
            put(slot, 0, "LowWeights", n)

    steps = []
    for s in range(SLOTS):
        if s < STEPS:
            steps.append((0, "Max", s))
        elif s < 2 * STEPS:
            steps.append((0, "Exp", s - STEPS))
        if 0 <= s - STEPS - MIX_LAG < STEPS:
            steps.append((0, "Mix", s - STEPS - MIX_LAG))
        steps += at[s]
    return steps


def stages_before():
    turns = [step for half in range(2) for step in ((0, "XTurn", half), (0, "XTurnLow", half))]
    projections = [[(0, name, m) for name in ("XProj", "XHigh", "XMid", "XLow")] for m in range(2 * DC)]
    values = [step for b in range(len(X_VAL_AT)) for step in ((0, "XVal", b), (0, "XValSum", b))]
    return [(0, "XStats"), (0, "XNorm"), (0, "Weights", 0), (0, "Ones"), *turns, (0, "XCtx"), (1, "XLoad"),
            projections[0][0], (0, "Absolute"), *projections[0][1:], (0, "Sums", 0), *projections[1], (0, "RowScale"),
            *projections[2], (0, "Inverse", 0), *projections[3], (0, "XStack", 0), (0, "XStack", 1), (0, "Inverse", 1),
            (0, "Weights", 1), (0, "Sums", 1), (0, "Inverse", 2), (0, "Scales"), (0, "Signs", 0),
            (0, "Signs", 1), *values, (0, "Inverse", 3), (1, "XStats"), (0, "OverHalf", 0),
            (0, "OverHalf", 1), (1, "XNorm")]


def stages_after():
    tail = [(0, name, SG - 1) for name, slot in LAST_TAIL]
    turns = [(0, name, half) for name in ("Turn3", "Turn3Low") for half in range(2)]
    ups = [(0, "Up", 0)] + [step for u in range(1, HC) for step in ((0, "Up", u), (0, "UpLow", u - 1))] + [(0, "UpLow", HC - 1)]
    downs = [step for b in range(SG) for step in ((0, "Down", 2 * b), (0, "Down", 2 * b + 1), (0, "Gain", b))]
    return [*tail, (0, "Stats2"), (0, "Norm2"), (0, "Keep"), *turns, (0, "LowRank"), (0, "LowRankLow"), *ups, *downs, (0, "Store")]


def walk(engine, stages):
    def run(g, steps):
        for distance, name, *arg in steps:
            if name in stages:
                stages[name](g + distance, *arg)

    run(0, stages_before())
    run(0, schedule(0, 2))
    with engine.Fori(1, GROUPS - 2) as g:
        run(g, schedule(1, 2))
    run(GROUPS - 2, schedule(1, 1))
    run(GROUPS - 1, schedule(1, 0))
    run(GROUPS - 1, stages_after())


def need(engine, sem, count):
    if isinstance(count, int) and count <= 0:
        return
    engine.wait_ge(sem, count)


def build_block(nc, x, ctx_t, mask, g_xattn, g_ffn, wq, bq, wk, bk, wv, bv, wo, bo,
                fast_b_t, w_fc_t, w_proj_t, u_t8, v, gate, out):
    with ExitStack() as stack:
        def sb(name, shape, dt):
            return stack.enter_context(nc.sbuf_tensor(name, shape, dt))

        def psum(name, shape):
            return stack.enter_context(nc.psum_tensor(name, shape, F32))

        def sem(name):
            return stack.enter_context(nc.semaphore(name))

        bank_score = psum("bank_score", [P, 2, 512])
        bank_mix = psum("bank_mix", [P, 512])
        bank_f = psum("bank_f", [P, 2, 512])
        bank_x = psum("bank_x", [P, 512])
        bank_t = psum("bank_t", [P, 2, 512])

        w_hi = sb("w_hi", [P, 4, DC, D], F32R)
        w_lo = sb("w_lo", [P, 4, DC, D], F32R)
        bias_qk = sb("bias_qk", [P, 2, DC], F32)
        bias_v = sb("bias_v", [P, D], F32)
        bias_o = sb("bias_o", [P, D], F32)
        gates = sb("gates", [P, 4], F32)
        fc_tern = sb("fc_tern", [P, DC, HID], F32R)
        fc_scale = sb("fc_scale", [P, HC], F32)
        pj_tern = sb("pj_tern", [P, HC, D], F32R)
        pj_scale = sb("pj_scale", [P, D], F32)
        pj_half = sb("pj_half", [P, D], F32)
        pj_gain = sb("pj_gain", [P, D], F32)
        v_in = sb("v_in", [RANK, D], F32)
        fb_in = sb("fb_in", [RANK, RANK], F32)
        fv = sb("fv", [P, DC, RANK], F32)
        fv_hi = sb("fv_hi", [P, DC, RANK], F32R)
        fv_rows = sb("fv_rows", [P, DC, P // RANK, RANK], F32R)
        u_rows = sb("u_rows", [P, HID], F32R)
        mask_in = sb("mask_in", [GROUPS, TOK], mask.dtype)
        mask_row = sb("mask_row", [GROUPS, TOK], BF16)
        ones = sb("ones", [P, P], F32)
        ident = sb("ident", [P, P], F32)
        ident16 = sb("ident16", [P, P], BF16)
        power = sb("power", [P, SG], F32)
        eps = sb("eps", [P, SG], F32)

        x_in = sb("x_in", [P, SG, D], F32)
        x_stat = sb("x_stat", [P, SG, 6], F32)
        x_mean = sb("x_mean", [P, SG, 2], F32)
        x_var = sb("x_var", [P, SG], F32)
        x_rstd = sb("x_rstd", [P, SG], F32)
        xt_hi = sb("xt_hi", [P, DC, TOK], F32R)
        xt_lo = sb("xt_lo", [P, DC, TOK], F32R)
        c_in = sb("c_in", [P, DC, TOK], F32)
        ct_hi = sb("ct_hi", [P, DC, TOK], F32R)
        ct_lo = sb("ct_lo", [P, DC, TOK], F32R)
        qk = sb("qk", [P, 2, TOK], F32)
        rest = sb("rest", [P, TOK], F32)
        parts = sb("parts", [P, 2 * DC, 3, TOK], BF16)
        vals = sb("vals", [P, SG, HEADS, STRIP], F32)
        q_stack = sb("q_stack", [P, HEADS, TOK], BF16)
        k_stack = sb("k_stack", [P, HEADS, TOK], BF16)
        maxima = sb("maxima", [P, SG, HEADS], F32)
        max_rest = sb("max_rest", [P, SG, HEADS], F32)
        max_parts = sb("max_parts", [P, SG, MAX_SLOTS, HEADS], BF16)
        hold = sb("hold", [P, 1], F32)
        max_rows = sb("max_rows", [3 * HEADS, TOK], BF16)
        probs = sb("probs", [P, PROB_BUFFERS, 4, SEQ], F32)
        mix_t = sb("mix_t", [P, 512], F32)
        denom = sb("denom", [P, HEADS], F32)
        attn = sb("attn", [P, D], F32)
        at_hi = sb("at_hi", [P, DC, SEQ], F32R)
        at_lo = sb("at_lo", [P, DC, SEQ], F32R)
        x1_and_norm = sb("x1_and_norm", [P, 2, SG, D], F32)
        x1, x1_norm = x1_and_norm[:, 0], x1_and_norm[:, 1]
        kept = sb("kept", [P, SG, D], F32)
        n_stat = sb("n_stat", [P, SG, 6], F32)
        n_mean = sb("n_mean", [P, SG, 2], F32)
        n_var = sb("n_var", [P, SG], F32)
        n_rstd = sb("n_rstd", [P, SG], F32)
        with ExitStack() as early:
            def early_sb(name, shape):
                return early.enter_context(nc.sbuf_tensor(name, shape, F32))

            fc_in = early_sb("fc_in", [P, DC, HID])
            pj_in = early_sb("pj_in", [P, HC, D])
            fc_abs = early_sb("fc_abs", [P, DC, HID])
            pj_abs = early_sb("pj_abs", [P, HC, D])
            half_scale = early_sb("half_scale", [P, 2, HID])
            scale_row = early_sb("scale_row", [P, HID])
            u_in = early_sb("u_in", [P, HID])
        sq_hi = sb("sq_hi", [P, HC, TOK], F32R)
        sq_lo = sb("sq_lo", [P, HC, TOK], F32R)
        nt_hi = sb("nt_hi", [P, DC, TOK], F32R)
        nt_lo = sb("nt_lo", [P, DC, TOK], F32R)
        relu = sb("relu", [P, 2, TOK], F32)
        square = sb("square", [P, 2, TOK], F32)
        low_rows = sb("low_rows", [P, TOK], F32R)
        y = sb("y", [P, 2, D], F32)
        w_in = x1_and_norm[:, :, :, :].rearrange("p a (w c) n -> p (a w) c n", c=DC)

        scratch_qk = nc.dram_tensor("scratch_qk", (2, 3, D, TOK), BF16, kind="Internal").ap()
        scratch_max = nc.dram_tensor("scratch_max", (3, HEADS, TOK), BF16, kind="Internal").ap()
        scratch_mask = nc.dram_tensor("scratch_mask", (GROUPS, TOK), BF16, kind="Internal").ap()

        w_loaded = [sem("wq_wk_loaded"), sem("wv_wo_loaded")]
        fc_loaded = sem("fc_loaded")
        small_loaded = sem("small_loaded")
        low_loaded = sem("low_loaded")
        mask_made = sem("mask_made")
        mask_written = sem("mask_written")
        consts_made = sem("consts_made")
        pool_consts = sem("pool_consts")
        wo_gated = sem("wo_gated")
        w_high = sem("w_high")
        w_split = sem("w_split")
        gates_made = sem("gates_made")
        abs_made = sem("abs_made")
        sums_made = sem("sums_made")
        signs_made = sem("signs_made")
        sums_read = sem("sums_read")
        row_scaled = sem("row_scaled")
        over_half = sem("over_half")
        scales_made = sem("scales_made")
        tern_made = sem("tern_made")
        low_made = sem("low_made")
        x_loaded = sem("x_loaded")
        c_loaded = sem("c_loaded")
        res_loaded = sem("res_loaded")
        x_counted = sem("x_counted")
        x_averaged = sem("x_averaged")
        x_var_made = sem("x_var_made")
        x_rstd_made = sem("x_rstd_made")
        x_normed = sem("x_normed")
        x_turned = sem("x_turned")
        xt_hi_made = sem("xt_hi_made")
        xt_lo_made = sem("xt_lo_made")
        ct_hi_made = sem("ct_hi_made")
        ct_lo_made = sem("ct_lo_made")
        qk_projected = sem("qk_projected")
        qk_biased = sem("qk_biased")
        part_high = sem("part_high")
        part_rest = sem("part_rest")
        part_mid = sem("part_mid")
        part_low = sem("part_low")
        parts_written = [sem(f"parts_written{m}") for m in range(2 * DC)]
        k_stacked = [sem(f"k_stacked{half}") for half in range(2)]
        q_stacked = [sem(f"q_stacked{half}") for half in range(2)]
        v_projected = sem("v_projected")
        vals_made = sem("vals_made")
        s1_done = sem("s1_done")
        max_taken = sem("max_taken")
        max_high = sem("max_high")
        max_rest_made = sem("max_rest_made")
        max_mid = sem("max_mid")
        max_split = sem("max_split")
        max_turned = sem("max_turned")
        max_rows_made = sem("max_rows_made")
        max_written = [sem(f"max_written{half}") for half in range(2)]
        max_loaded = [sem(f"max_loaded{half}") for half in range(2)]
        s2_done = sem("s2_done")
        exp_done = sem("exp_done")
        mix_done = sem("mix_done")
        mix_evicted = sem("mix_evicted")
        mix_turned = sem("mix_turned")
        denom_made = sem("denom_made")
        attn_made = sem("attn_made")
        attn_turned = sem("attn_turned")
        at_hi_made = sem("at_hi_made")
        at_lo_made = sem("at_lo_made")
        o_projected = sem("o_projected")
        res_biased = sem("res_biased")
        x1_made = sem("x1_made")
        n_counted = sem("n_counted")
        n_averaged = sem("n_averaged")
        n_var_made = sem("n_var_made")
        n_rstd_made = sem("n_rstd_made")
        x1_normed = sem("x1_normed")
        x1_kept = sem("x1_kept")
        x1_turned = sem("x1_turned")
        nt_hi_made = sem("nt_hi_made")
        nt_lo_made = sem("nt_lo_made")
        low_summed = sem("low_summed")
        low_hi_made = sem("low_hi_made")
        low_lo_made = sem("low_lo_made")
        up_done = sem("up_done")
        relu_made = sem("relu_made")
        sq_hi_made = sem("sq_hi_made")
        square_made = sem("square_made")
        sq_lo_made = sem("sq_lo_made")
        down_done = sem("down_done")
        y_made = sem("y_made")
        out_made = sem("out_made")
        stored = sem("stored")

        SMALL_LOADS, LOW_LOADS, POOL_CONSTS, STACK_CONSTS = 8, 3, 6, 3
        stack_k_loads = len(K_PARTS) + 1
        stack_q_loads = len(Q_PARTS)
        FV_COL = D + HC

        block = stack.enter_context(nc.Block())

        @block.sync
        def _(sp):
            def x_load(g):
                need(sp, x_turned, 2 * g)
                sp.dma_start(x_in[:, :, :], x[bass.ds(SG * g, SG)].rearrange("b p d -> p b d")).then_inc(x_loaded, 16)
                need(sp, ct_lo_made, g)
                sp.dma_start(c_in[:, :, :], ctx_t[:, bass.ds(TOK * g, TOK)].rearrange("(c p) t -> p c t", p=P)
                             ).then_inc(c_loaded, 16)

            def load(g):
                need(sp, x1_kept, g)
                if isinstance(g, int) and g == 0:
                    sp.wait_ge(w_split, 2)
                sp.dma_start(x1[:, :, :], x[bass.ds(SG * g, SG)].rearrange("b p d -> p b d")).then_inc(res_loaded, 16)

            def shift(g, half):
                cols = slice(half * TOK // 2, (half + 1) * TOK // 2)
                sp.wait_ge(max_rows_made, 2 * g + half + 1)
                sp.dma_start(scratch_max.rearrange("n h t -> (n h) t")[:, cols], max_rows[:, cols]
                             ).then_inc(max_written[half], 16)
                sp.wait_ge(max_written[half], 16 * (g + 1))
                sp.dma_start(q_stack[ROW_MAX:ROW_MAX + 3, :, cols], scratch_max[:, :, cols]
                             ).then_inc(max_loaded[half], 16)

            def x_proj(g, m):
                sp.wait_ge(part_low, 2 * DC * g + m + 1)
                sp.dma_start(scratch_qk[m // DC].rearrange("n (c p) t -> c p n t", p=P)[m % DC],
                             parts[:, m, :, :]).then_inc(parts_written[m], 16)

            def x_stack(g, half):
                cols = slice(half * TOK // 2, (half + 1) * TOK // 2)
                need(sp, s2_done, STEPS * (g - 1) + (half + 1) * STEPS // 2)
                row = scratch_mask[bass.ds(g, 1), cols]
                sp.dma_start(k_stack[ROW_MASK:ROW_MASK + 1, :, cols],
                             row.unsqueeze(1).to_broadcast([1, HEADS, TOK // 2])).then_inc(k_stacked[half], 16)
                for which, names, tile, done in ((0, Q_PARTS, q_stack, q_stacked), (1, K_PARTS, k_stack, k_stacked)):
                    if half == 0:
                        for c in range(DC):
                            sp.wait_ge(parts_written[DC * which + c], 16 * (g + 1))
                    for n, part in enumerate(names):
                        sp.dma_start(tile[DEPTH * n:DEPTH * (n + 1), :, cols],
                                     scratch_qk[which, part, :, cols].rearrange("(h d) t -> d h t", d=DEPTH)
                                     ).then_inc(done[half], 16)

            def store(g):
                sp.wait_ge(out_made, SG * (g + 1))
                sp.dma_start(out[bass.ds(SG * g, SG)].rearrange("b p d -> p b d"), kept[:, :, :]).then_inc(stored, 16)

            def load_weights(half):
                for n in (2 * half, 2 * half + 1):
                    sp.dma_start(w_in[:, n, :, :], (wq, wk, wv, wo)[n].rearrange("(c p) n -> p c n", p=P)
                                 ).then_inc(w_loaded[half], 16)

            sp.dma_start(x_in[:, :, :], x[0:SG].rearrange("b p d -> p b d")).then_inc(x_loaded, 16)
            load_weights(0)
            for n, b in enumerate((bq, bk)):
                sp.dma_start(bias_qk[:, n, :], b).then_inc(small_loaded, 16)
            for n, s in enumerate((g_xattn, g_ffn, gate)):
                sp.dma_start(gates[:, n:n + 1], s.partition_broadcast(P)).then_inc(small_loaded, 16)
            for tile, b in ((bias_v, bv), (bias_o, bo)):
                sp.dma_start(tile[:, :], b.partition_broadcast(P)).then_inc(small_loaded, 16)
            sp.dma_start(mask_in[:, :], mask.rearrange("(g s) k -> g (s k)", s=SG)).then_inc(small_loaded, 16)
            sp.dma_start(c_in[:, :, :], ctx_t[:, 0:TOK].rearrange("(c p) t -> p c t", p=P)).then_inc(c_loaded, 16)
            load_weights(1)
            sp.dma_start(fc_in[:, :, :], w_fc_t.rearrange("(c p) n -> p c n", p=P)).then_inc(fc_loaded, 16)
            sp.dma_start(pj_in[:, :, :], w_proj_t.rearrange("(c p) n -> p c n", p=P)).then_inc(fc_loaded, 16)
            sp.dma_start(v_in[:, :], v).then_inc(low_loaded, 16)
            sp.dma_start(fb_in[:, :], fast_b_t).then_inc(low_loaded, 16)
            sp.dma_start(u_in[:, :], u_t8).then_inc(low_loaded, 16)
            sp.wait_ge(mask_made, 1)
            sp.dma_start(scratch_mask, mask_row[:, :]).then_inc(mask_written, 16)
            sp.wait_ge(consts_made, STACK_CONSTS)
            sp.wait_ge(mask_written, 16)

            walk(sp, {"XLoad": x_load, "Load": load, "ShiftTurn": shift, "XLow": x_proj, "XStack": x_stack, "Store": store})
            sp.wait_ge(stored, 16 * GROUPS)

        @block.tensor
        def _(pe):
            def split_product(dst, pairs):
                for n, (lhs, rhs) in enumerate(pairs):
                    mm = pe.matmul(dst, lhs, rhs, start=n == 0, stop=n == len(pairs) - 1)
                return mm

            def sums(g, step):
                if step == 0:
                    pe.wait_ge(abs_made, 1)
                    pe.wait_ge(consts_made, 1)
                    for n in range(2):
                        mm = split_product(bank_f[:, n, :], [(ones[:, :], fc_abs[:, c, n * 512:(n + 1) * 512]) for c in range(DC)])
                    mm.then_inc(sums_made, 1)
                    return
                pe.wait_ge(abs_made, 2)
                split_product(bank_mix[:, 0:D], [(ones[:, :], pj_abs[:, c, :]) for c in range(HC)])
                for u in range(HC):
                    split_product(bank_mix[:, D + u:D + u + 1],
                                  [(fc_abs[:, c, u * P:(u + 1) * P], ones[:, 0:1]) for c in range(DC)])
                pe.wait_ge(low_loaded, 16 * LOW_LOADS)
                for c in range(DC):
                    mm = pe.matmul(bank_mix[:, FV_COL + c * RANK:FV_COL + (c + 1) * RANK], v_in[:, c * P:(c + 1) * P],
                                   fb_in[:, :], start=True, stop=True)
                mm.then_inc(sums_made, 1)

            def x_turn(g, half):
                pe.wait_ge(x_normed, SG * g + 2 * half + 2)
                if half == 0:
                    need(pe, vals_made, SG * g)
                else:
                    pe.wait_ge(xt_lo_made, 2 * g + 1)
                for c in range(DC):
                    for n in range(2):
                        mm = pe.transpose(bank_x[:, (2 * c + n) * P:(2 * c + n + 1) * P],
                                          x_in[:, 2 * half + n, c * P:(c + 1) * P], ident[:, :])
                mm.then_inc(x_turned, 1)

            def x_proj(g, m):
                which, c = m // DC, m % DC
                hi, lo = (xt_hi, xt_lo) if which == 0 else (ct_hi, ct_lo)
                if m == 0:
                    pe.wait_ge(xt_lo_made, 2 * g + 2)
                    need(pe, w_split, 1)
                else:
                    pe.wait_ge(qk_biased, 2 * DC * g + m)
                if m == DC:
                    pe.wait_ge(ct_hi_made, g + 1)
                    pe.wait_ge(ct_lo_made, g + 1)
                cols = slice(c * P, (c + 1) * P)
                split_product(bank_x[:, :], [(w[:, which, k, cols], t[:, k, :])
                                             for w, t in ((w_hi, hi), (w_lo, hi), (w_hi, lo)) for k in range(DC)]
                              ).then_inc(qk_projected, 1)

            def x_val(g, b):
                if b == 0:
                    pe.wait_ge(qk_biased, 2 * DC * (g + 1))
                    need(pe, w_split, 2)
                else:
                    pe.wait_ge(vals_made, SG * g + b)
                toks = slice(b * SEQ, (b + 1) * SEQ)
                split_product(bank_x[:, 0:D], [(t[:, k, toks], w[:, 2, k, :])
                                               for w, t in ((w_hi, ct_hi), (w_lo, ct_hi), (w_hi, ct_lo)) for k in range(DC)]
                              ).then_inc(v_projected, 1)

            def max_scores(g, s):
                b, quarter = s // QUARTERS, s % QUARTERS
                if s % (STEPS // 2) == 0:
                    half = 2 * s // STEPS
                    pe.wait_ge(q_stacked[half], 16 * stack_q_loads * (g + 1))
                    pe.wait_ge(k_stacked[half], 16 * stack_k_loads * (g + 1))
                if s < 2:
                    need(pe, exp_done, STEPS * g - 1 + s)
                else:
                    pe.wait_ge(max_taken, STEPS * g + s - 1)
                toks = slice(b * SEQ, (b + 1) * SEQ)
                for n in range(4):
                    h = 4 * quarter + n
                    mm = pe.matmul(bank_score[:, s % 2, n * SEQ:(n + 1) * SEQ], q_stack[0:ROWS_S1, h, toks],
                                   k_stack[0:ROWS_S1, h, toks], start=True, stop=True)
                mm.then_inc(s1_done, 1)

            def shift(g, half):
                pe.wait_ge(max_split, 2 * g + half + 1)
                if half == 0:
                    need(pe, nt_lo_made, 2 * g)
                else:
                    pe.wait_ge(max_rows_made, 2 * g + 1)
                rows = bank_t[0:MAX_SLOTS * HEADS, 0, 0:TOK // 2].bitcast(BF16)
                for b in range(2 * half, 2 * half + 2):
                    mm = pe.transpose(rows[:, b * SEQ:(b + 1) * SEQ],
                                      max_parts[:, b, :, :].rearrange("p n h -> p (n h)"), ident16[:, :])
                mm.then_inc(max_turned, 1)

            def exp_scores(g, s):
                b, quarter = s // QUARTERS, s % QUARTERS
                if s % (STEPS // 2) == 0:
                    pe.wait_ge(max_loaded[2 * s // STEPS], 16 * (g + 1))
                if s < 2:
                    pe.wait_ge(max_taken, STEPS * g + STEPS - 1 + s)
                else:
                    pe.wait_ge(exp_done, STEPS * g + s - 1)
                toks = slice(b * SEQ, (b + 1) * SEQ)
                for n in range(4):
                    h = 4 * quarter + n
                    mm = pe.matmul(bank_score[:, s % 2, n * SEQ:(n + 1) * SEQ], k_stack[0:ROWS_S2, h, toks],
                                   q_stack[0:ROWS_S2, h, toks], start=True, stop=True)
                mm.then_inc(s2_done, 1)

            def mix(g, s):
                b, quarter = s // QUARTERS, s % QUARTERS
                pe.wait_ge(exp_done, STEPS * g + s + 1)
                if quarter == 0:
                    pe.wait_ge(vals_made, SG * g + b + 1)
                    need(pe, mix_evicted, SG * g + b)
                    if isinstance(g, int) and g == 0:
                        pe.wait_ge(sums_read, 1)
                for n in range(4):
                    mm = pe.matmul(bank_mix[STRIP * n:STRIP * (n + 1), quarter * SEQ:(quarter + 1) * SEQ],
                                   vals[:, b, 4 * quarter + n, :], probs[:, s % PROB_BUFFERS, n, :], start=True, stop=True)
                mm.then_inc(mix_done, 1)

            def turn4(g, b):
                pe.wait_ge(mix_evicted, SG * g + b + 1)
                if b == 0:
                    pe.wait_ge(max_rows_made, 2 * g + 2)
                else:
                    pe.wait_ge(x1_made, SG * g + b)
                for n in range(QUARTERS):
                    mm = pe.transpose(bank_t[:, 0, n * P:(n + 1) * P], mix_t[:, n * P:(n + 1) * P], ident[:, :])
                mm.then_inc(mix_turned, 1)

            def turn2(g, b):
                pe.wait_ge(attn_made, SG * g + b + 1)
                if b == 0:
                    need(pe, nt_lo_made, 2 * g)
                else:
                    pe.wait_ge(at_lo_made, SG * g + b)
                for c in range(DC):
                    mm = pe.transpose(bank_t[:, 1, c * P:(c + 1) * P], attn[:, c * P:(c + 1) * P], ident[:, :])
                mm.then_inc(attn_turned, 1)

            def out_proj(g, b):
                pe.wait_ge(at_lo_made, SG * g + b + 1)
                split_product(bank_t[:, 0, 0:D], [(t[:, k, :], w[:, 3, k, :])
                                                  for w, t in ((w_hi, at_hi), (w_lo, at_hi), (w_hi, at_lo)) for k in range(DC)]
                              ).then_inc(o_projected, 1)

            def turn3(g, pair):
                pe.wait_ge(x1_normed, SG * g + 2 * pair + 2)
                pe.wait_ge(at_lo_made, SG * (g + 1))
                for c in range(DC):
                    for n in range(2):
                        mm = pe.transpose(bank_t[:, 1 - pair, (2 * c + n) * P:(2 * c + n + 1) * P],
                                          x1_norm[:, 2 * pair + n, c * P:(c + 1) * P], ident[:, :])
                mm.then_inc(x1_turned, 1)

            def low_rank(g):
                pe.wait_ge(nt_lo_made, 2 * (g + 1))
                need(pe, low_made, 2)
                split_product(bank_f[:, 0, :], [(fv_rows[:, k, :, :].rearrange("p a r -> p (a r)"), t[:, k, :])
                                                for t in (nt_hi, nt_lo) for k in range(DC)]).then_inc(low_summed, 1)

            def up(g, u):
                cols = slice(u * P, (u + 1) * P)
                if u == 1:
                    pe.wait_ge(low_lo_made, g + 1)
                elif u > 1:
                    pe.wait_ge(relu_made, HC * g + u - 1)
                dst = bank_f[:, (u + 1) % 2, :]
                if u == 0:
                    need(pe, tern_made, 2)
                for n, (t, k) in enumerate((t, k) for t in (nt_hi, nt_lo) for k in range(DC)):
                    pe.matmul(dst, fc_tern[:, k, cols], t[:, k, :], start=n == 0, stop=False)
                if u == 0:
                    pe.wait_ge(low_lo_made, g + 1)
                pe.matmul(dst, u_rows[:, cols], low_rows[:, :], start=False, stop=True).then_inc(up_done, 1)

            def down(g, n):
                b, half = n // 2, n % 2
                toks = slice(b * SEQ, (b + 1) * SEQ)
                dst = bank_f[:, (b + 1) % 2, 0:D]
                if n == 0:
                    pe.wait_ge(relu_made, HC * g + HC - 1)
                elif n == 2:
                    pe.wait_ge(relu_made, HC * g + HC)
                elif half == 0:
                    pe.wait_ge(y_made, SG * g + b - 1)
                for u in range(half * HC // 2, (half + 1) * HC // 2):
                    if b == 0:
                        pe.wait_ge(sq_lo_made, HC * g + u + 1)
                        pe.wait_ge(sq_hi_made, HC * g + u + 1)
                    pe.matmul(dst, sq_hi[:, u, toks], pj_tern[:, u, :], start=u == 0, stop=False)
                    mm = pe.matmul(dst, sq_lo[:, u, toks], pj_tern[:, u, :], start=False, stop=u == HC - 1)
                if half == 1:
                    mm.then_inc(down_done, 1)

            pe.wait_ge(pool_consts, POOL_CONSTS)
            walk(pe, {"Sums": sums, "XTurn": x_turn, "XProj": x_proj, "XVal": x_val, "Max": max_scores, "ShiftTurn": shift,
                      "Exp": exp_scores, "Mix": mix, "Turn4": turn4, "Turn2": turn2, "Out": out_proj,
                      "Turn3": turn3, "LowRank": low_rank, "Up": up, "Down": down})

        @block.scalar
        def _(act):
            def weights(g, half):
                pair = slice(2 * half, 2 * half + 2)
                act.wait_ge(w_loaded[half], 32)
                if half == 1:
                    act.wait_ge(wo_gated, 1)
                act.activation(w_hi[:, pair, :, :], w_in[:, pair, :, :], ACT.Copy).then_inc(w_high, 1)
                if half == 0:
                    act.wait_ge(small_loaded, 16 * SMALL_LOADS)
                    act.activation(gates[:, 0:2], gates[:, 0:2], ACT.Tanh).then_inc(gates_made, 1)

            def absolute(g):
                act.wait_ge(fc_loaded, 32)
                for w, w_abs in ((fc_in, fc_abs), (pj_in, pj_abs)):
                    act.activation(w_abs[:, :, :], w[:, :, :], ACT.Abs).then_inc(abs_made, 1)

            def signs(g, n):
                w = (fc_in, pj_in)[n]
                act.wait_ge(abs_made, 2)
                act.activation(w[:, :, :], w[:, :, :], ACT.Sign).then_inc(signs_made, 1)

            def x_turn(g, half):
                act.wait_ge(x_turned, 2 * g + half + 1)
                need(act, qk_projected, 2 * DC * g)
                act.activation(xt_hi[:, :, 2 * half * SEQ:2 * (half + 1) * SEQ],
                               bank_x[:, :].rearrange("p (c t) -> p c t", c=DC), ACT.Copy).then_inc(xt_hi_made, 1)

            def x_ctx(g):
                act.wait_ge(c_loaded, 16 * (g + 1))
                need(act, v_projected, SG * g)
                act.activation(ct_hi[:, :, :], c_in[:, :, :], ACT.Copy).then_inc(ct_hi_made, 1)

            def x_proj(g, m):
                act.wait_ge(qk_projected, 2 * DC * g + m + 1)
                need(act, part_rest, 2 * DC * g + m - 1)
                act.activation(qk[:, m % 2, :], bank_x[:, :], ACT.Identity,
                               bias=bias_qk[:, m // DC, m % DC:m % DC + 1]).then_inc(qk_biased, 1)

            def x_mid(g, m):
                act.wait_ge(part_rest, 2 * DC * g + m + 1)
                act.activation(parts[:, m, 1, :], rest[:, :], ACT.Copy).then_inc(part_mid, 1)

            def shift(g, half):
                cols = slice(half * TOK // 2, (half + 1) * TOK // 2)
                act.wait_ge(max_turned, 2 * g + half + 1)
                need(act, max_written[half], 16 * g)
                act.activation(max_rows[:, cols], bank_t[0:3 * HEADS, 0, 0:TOK // 2].bitcast(BF16)[:, cols], ACT.Copy
                               ).then_inc(max_rows_made, 1)

            def exp_scores(g, s):
                act.wait_ge(s2_done, STEPS * g + s + 1)
                need(act, mix_done, STEPS * g + max(0, s + 1 - PROB_BUFFERS))
                act.activation(probs[:, s % PROB_BUFFERS, :, :].rearrange("p n t -> p (n t)"), bank_score[:, s % 2, :], ACT.Exp,
                               scale=float(DEPTH) ** -0.5).then_inc(exp_done, 1)

            def turn2(g, b):
                act.wait_ge(attn_turned, SG * g + b + 1)
                need(act, o_projected, SG * g + b)
                act.activation(at_hi[:, :, :], bank_t[:, 1, 0:D].rearrange("p (c t) -> p c t", c=DC), ACT.Copy
                               ).then_inc(at_hi_made, 1)

            def keep(g):
                act.wait_ge(x1_normed, SG * (g + 1))
                need(act, stored, 16 * g)
                act.activation(kept[:, :, :], x1[:, :, :], ACT.Copy).then_inc(x1_kept, 1)
                if isinstance(g, int) and g == 0:
                    act.wait_ge(low_made, 2)

            def turn3(g, pair):
                act.wait_ge(x1_turned, 2 * g + pair + 1)
                act.activation(nt_hi[:, :, 2 * pair * SEQ:2 * (pair + 1) * SEQ],
                               bank_t[:, 1 - pair, :].rearrange("p (c t) -> p c t", c=DC), ACT.Copy
                               ).then_inc(nt_hi_made, 1)

            def low_rank(g):
                act.wait_ge(low_summed, g + 1)
                act.activation(low_rows[:, :], bank_f[:, 0, :], ACT.Copy).then_inc(low_hi_made, 1)

            def up(g, u):
                act.wait_ge(up_done, HC * g + u + 1)
                if u >= 2:
                    act.wait_ge(square_made, HC * g + u - 1)
                act.activation(relu[:, u % 2, :], bank_f[:, (u + 1) % 2, :], ACT.Relu, scale=fc_scale[:, u:u + 1]
                               ).then_inc(relu_made, 1)
                act.wait_ge(relu_made, HC * g + u + 1)
                act.activation(sq_hi[:, u, :], relu[:, u % 2, :], ACT.Square).then_inc(sq_hi_made, 1)

            walk(act, {"Weights": weights, "Absolute": absolute, "Signs": signs, "XTurn": x_turn, "XCtx": x_ctx,
                       "XProj": x_proj, "XMid": x_mid, "ShiftTurn": shift, "Exp": exp_scores, "Turn2": turn2,
                       "Keep": keep, "Turn3": turn3, "LowRank": low_rank, "Up": up})

        @block.vector
        def _(dve):
            def weights(g, half):
                pair = slice(2 * half, 2 * half + 2)
                if half == 0:
                    dve.wait_ge(small_loaded, 16 * SMALL_LOADS)
                    dve.tensor_scalar(mask_row[:, :], mask_in[:, :], MASKED, MASKED, ALU.mult, ALU.subtract
                                      ).then_inc(mask_made, 1)
                else:
                    dve.wait_ge(w_loaded[1], 32)
                    dve.wait_ge(gates_made, 1)
                    dve.tensor_scalar(w_in[:, 3, :, :], w_in[:, 3, :, :], gates[:, 0:1], None, ALU.mult).then_inc(wo_gated, 1)
                    dve.tensor_scalar(bias_o[:, :], bias_o[:, :], gates[:, 0:1], None, ALU.mult).then_inc(gates_made, 1)
                dve.wait_ge(w_high, half + 1)
                dve.tensor_tensor(w_lo[:, pair, :, :], w_in[:, pair, :, :], w_hi[:, pair, :, :].bitcast(F32), ALU.subtract
                                  ).then_inc(w_split, 1)

            def scales(g):
                dve.wait_ge(sums_made, 2)
                dve.tensor_scalar(fc_scale[:, :], bank_mix[:, D:D + HC], 1.0 / D, SCALE_MIN, ALU.mult, ALU.max)
                dve.tensor_scalar(pj_scale[:, :], bank_mix[:, 0:D], 1.0 / HID, SCALE_MIN, ALU.mult, ALU.max)
                dve.tensor_copy(fv[:, :, :], bank_mix[:, FV_COL:FV_COL + DC * RANK].rearrange("p (c r) -> p c r", c=DC)
                                ).then_inc(sums_read, 1)
                dve.wait_ge(sums_read, 1)
                dve.tensor_scalar(pj_half[:, :], pj_scale[:, :], 0.5, None, ALU.mult).then_inc(row_scaled, 1)
                dve.tensor_scalar(pj_gain[:, :], pj_scale[:, :], gates[:, 1:2], None, ALU.mult)

            def row_scale(g):
                dve.wait_ge(sums_made, 1)
                dve.tensor_scalar(scale_row[:, :], bank_f[:, :, :].rearrange("p a n -> p (a n)"), 1.0 / D, SCALE_MIN,
                                  ALU.mult, ALU.max).then_inc(row_scaled, 1)
                dve.wait_ge(row_scaled, 1)
                dve.tensor_scalar(half_scale[:, 0, :], scale_row[:, :], 0.5, None, ALU.mult).then_inc(row_scaled, 1)

            def inverse(g, n):
                cols = slice(n * HID // 4, (n + 1) * HID // 4)
                dve.reciprocal(half_scale[:, 1, cols], scale_row[:, cols]).then_inc(scales_made, 1)

            def over(g, n):
                dve.wait_ge(row_scaled, 3)
                if n < 2:
                    dve.tensor_tensor(fc_abs[:, n, :], fc_abs[:, n, :], half_scale[:, 0, :], ALU.is_gt).then_inc(over_half, 1)
                else:
                    cs = slice((n - 2) * HC // 2, (n - 1) * HC // 2)
                    dve.tensor_tensor(pj_abs[:, cs, :], pj_abs[:, cs, :],
                                      pj_half[:, :].unsqueeze(1).to_broadcast([P, HC // 2, D]), ALU.is_gt).then_inc(over_half, 1)

            def low_weights(g, step):
                if step == 0:
                    dve.wait_ge(low_loaded, 16 * LOW_LOADS)
                    dve.tensor_scalar(u_in[:, :], u_in[:, :], gates[:, 2:3], None, ALU.mult).then_inc(scales_made, 1)
                    dve.tensor_copy(fv_hi[:, :, :], fv[:, :, :]).then_inc(scales_made, 1)
                elif step == 1:
                    dve.wait_ge(scales_made, 6)
                    dve.tensor_tensor(u_in[:, :], u_in[:, :], half_scale[:, 1, :], ALU.mult).then_inc(scales_made, 1)
                    for a in range(0, P // RANK, 2):
                        dve.tensor_copy(fv_rows[:, :, a, :], fv_hi[:, :, :].bitcast(F32))
                        dve.tensor_tensor(fv_rows[:, :, a + 1, :], fv[:, :, :], fv_hi[:, :, :].bitcast(F32), ALU.subtract)
                else:
                    dve.wait_ge(scales_made, 7)
                    dve.tensor_copy(u_rows[:, :], u_in[:, :]).then_inc(low_made, 1)
                    dve.wait_ge(low_made, 1)
                    for q in (1, 3):
                        rows = slice(32 * q, 32 * (q + 1))
                        last = dve.tensor_tensor(u_rows[rows, :], u_in[rows, :], u_rows[rows, :].bitcast(F32), ALU.subtract)
                    last.then_inc(low_made, 1)

            def x_stats(g):
                dve.wait_ge(x_loaded, 16 * (g + 1))
                need(dve, x_rstd_made, g)
                for b in range(SG):
                    last = dve.bn_stats(x_stat[:, b, :], x_in[:, b, :])
                last.then_inc(x_counted, 1)
                dve.wait_ge(x_counted, g + 1)
                dve.memset(hold[:, :], 0.0)
                for b in range(SG):
                    last = dve.bn_aggr(x_mean[:, b, :], x_stat[:, b, :])
                last.then_inc(x_averaged, 1)

            def x_normalise(g):
                dve.wait_ge(x_rstd_made, g + 1)
                for b in range(SG):
                    dve.tensor_scalar(x_in[:, b, :], x_in[:, b, :], x_mean[:, b, 0:1], x_rstd[:, b:b + 1],
                                      ALU.subtract, ALU.mult).then_inc(x_normed, 1)

            def x_turn(g, half):
                dve.wait_ge(xt_hi_made, 2 * g + half + 1)
                cols = slice(2 * half * SEQ, 2 * (half + 1) * SEQ)
                dve.tensor_tensor(xt_lo[:, :, cols], bank_x[:, :].rearrange("p (c t) -> p c t", c=DC),
                                  xt_hi[:, :, cols].bitcast(F32), ALU.subtract).then_inc(xt_lo_made, 1)

            def x_proj(g, m):
                dve.wait_ge(qk_biased, 2 * DC * g + m + 1)
                need(dve, parts_written[m], 16 * g)
                dve.tensor_copy(parts[:, m, 0, :], qk[:, m % 2, :]).then_inc(part_high, 1)

            def x_val(g, b):
                dve.wait_ge(v_projected, SG * g + b + 1)
                if isinstance(g, int) and g == 0:
                    dve.wait_ge(pool_consts, POOL_CONSTS)
                else:
                    need(dve, mix_done, STEPS * (g - 1) + QUARTERS * (b + 1))
                dve.tensor_tensor(vals[:, b, :, 0:DEPTH], bank_x[:, 0:D].rearrange("p (h d) -> p h d", h=HEADS),
                                  bias_v[:, :].rearrange("p (h d) -> p h d", h=HEADS), ALU.add).then_inc(vals_made, 1)

            def take_max(g, s):
                b, quarter = s // QUARTERS, s % QUARTERS
                dve.wait_ge(s1_done, STEPS * g + s + 1)
                dve.tensor_reduce(maxima[:, b, 4 * quarter:4 * quarter + 4],
                                  bank_score[:, s % 2, :].rearrange("p (n k) -> p n k", n=4), AX_X, ALU.max
                                  ).then_inc(max_taken, 1)

            def shift(g, half):
                bs = slice(2 * half, 2 * half + 2)
                done = 2 * g + half + 1
                dve.wait_ge(max_taken, STEPS * g + (half + 1) * STEPS // 2)
                need(dve, max_turned, 2 * g)
                dve.tensor_scalar(max_parts[:, bs, 0, :], maxima[:, bs, :], -1.0, None, ALU.mult).then_inc(max_high, 1)
                dve.wait_ge(max_high, done)
                dve.scalar_tensor_tensor(max_rest[:, bs, :], maxima[:, bs, :], -1.0, max_parts[:, bs, 0, :], ALU.mult,
                                         ALU.subtract).then_inc(max_rest_made, 1)
                dve.wait_ge(max_rest_made, done)
                dve.tensor_copy(max_parts[:, bs, 1, :], max_rest[:, bs, :]).then_inc(max_mid, 1)
                dve.wait_ge(max_mid, done)
                dve.tensor_tensor(max_parts[:, bs, 2, :], max_rest[:, bs, :], max_parts[:, bs, 1, :], ALU.subtract
                                  ).then_inc(max_split, 1)

            def evict(g, b):
                dve.wait_ge(mix_done, STEPS * g + QUARTERS * (b + 1))
                need(dve, mix_turned, SG * g + b)
                dve.tensor_copy(mix_t[:, :], bank_mix[:, :]).then_inc(mix_evicted, 1)

            def turn4(g, b):
                heads = bank_t[:, 0, :].rearrange("p (h e) -> p h e", h=HEADS)
                dve.wait_ge(mix_turned, SG * g + b + 1)
                dve.reciprocal(denom[:, :], heads[:, :, DEPTH]).then_inc(denom_made, 1)
                dve.wait_ge(denom_made, SG * g + b + 1)
                need(dve, attn_turned, SG * g + b)
                dve.tensor_tensor(attn[:, :].rearrange("p (h d) -> p h d", h=HEADS), heads[:, :, 0:DEPTH],
                                  denom[:, :].unsqueeze(2).to_broadcast([P, HEADS, DEPTH]), ALU.mult).then_inc(attn_made, 1)

            def turn2(g, b):
                dve.wait_ge(at_hi_made, SG * g + b + 1)
                dve.tensor_tensor(at_lo[:, :, :], bank_t[:, 1, 0:D].rearrange("p (c t) -> p c t", c=DC),
                                  at_hi[:, :, :].bitcast(F32), ALU.subtract).then_inc(at_lo_made, 1)

            def out_proj(g, b):
                dve.wait_ge(o_projected, SG * g + b + 1)
                dve.wait_ge(res_biased, g + 1)
                dve.tensor_tensor(x1[:, b, :], bank_t[:, 0, 0:D], x1[:, b, :], ALU.add).then_inc(x1_made, 1)
                dve.wait_ge(x1_made, SG * g + b + 1)
                need(dve, n_averaged, g)
                dve.bn_stats(n_stat[:, b, :], x1[:, b, :]).then_inc(n_counted, 1)

            def stats2(g):
                dve.wait_ge(n_counted, SG * (g + 1))
                dve.memset(hold[:, :], 0.0)
                for b in range(SG):
                    last = dve.bn_aggr(n_mean[:, b, :], n_stat[:, b, :])
                last.then_inc(n_averaged, 1)

            def norm2(g):
                dve.wait_ge(n_rstd_made, g + 1)
                need(dve, x1_turned, 2 * g)
                for b in range(SG):
                    dve.tensor_scalar(x1_norm[:, b, :], x1[:, b, :], n_mean[:, b, 0:1], n_rstd[:, b:b + 1],
                                      ALU.subtract, ALU.mult).then_inc(x1_normed, 1)

            def turn3(g, pair):
                dve.wait_ge(nt_hi_made, 2 * g + pair + 1)
                toks = slice(2 * pair * SEQ, 2 * (pair + 1) * SEQ)
                dve.tensor_tensor(nt_lo[:, :, toks], bank_t[:, 1 - pair, :].rearrange("p (c t) -> p c t", c=DC),
                                  nt_hi[:, :, toks].bitcast(F32), ALU.subtract).then_inc(nt_lo_made, 1)

            def low_rank(g):
                dve.wait_ge(low_hi_made, g + 1)
                dve.tensor_tensor(low_rows[64:P, :], bank_f[64:P, 0, :], low_rows[64:P, :].bitcast(F32), ALU.subtract
                                  ).then_inc(low_lo_made, 1)

            def up(g, u):
                dve.wait_ge(square_made, HC * g + u + 1)
                dve.wait_ge(sq_hi_made, HC * g + u + 1)
                dve.tensor_tensor(sq_lo[:, u, :], square[:, u % 2, :], sq_hi[:, u, :].bitcast(F32), ALU.subtract
                                  ).then_inc(sq_lo_made, 1)

            def down(g, b):
                dve.wait_ge(down_done, SG * g + b + 1)
                if b >= 2:
                    dve.wait_ge(out_made, SG * g + b - 1)
                dve.tensor_tensor(y[:, b % 2, :], bank_f[:, (b + 1) % 2, 0:D], pj_gain[:, :], ALU.mult).then_inc(y_made, 1)

            dve.memset(max_parts[:, :, :, :], 0.0)
            dve.memset(ones[:, :], 1.0).then_inc(consts_made, 1)
            walk(dve, {"Weights": weights, "Scales": scales, "RowScale": row_scale, "Inverse": inverse, "OverHalf": over, "LowWeights": low_weights, "XStats": x_stats, "XNorm": x_normalise, "XTurnLow": x_turn,
                       "XHigh": x_proj, "XValSum": x_val, "Max": take_max, "Shift": shift, "Evict": evict, "Norm4": turn4,
                       "Turn2Low": turn2, "OutSum": out_proj, "Stats2": stats2, "Norm2": norm2, "Turn3Low": turn3,
                       "LowRankLow": low_rank, "UpLow": up, "Gain": down})

        @block.gpsimd
        def _(pool):
            def ones_rows(g):
                pool.wait_ge(pool_consts, POOL_CONSTS)
                pool.wait_ge(x_rstd_made, 1)
                pool.memset(q_stack[ROWS_QK:P, :, :].bitcast(F32), TWO_ONES).then_inc(consts_made, 1)
                pool.wait_ge(consts_made, 2)
                pool.memset(k_stack[ROWS_QK:P, :, :].bitcast(F32), TWO_ONES).then_inc(consts_made, 1)
                pool.wait_ge(consts_made, STACK_CONSTS)

            def ternary(g, n):
                tern, w_sign, over = ((fc_tern, fc_in, fc_abs), (pj_tern, pj_in, pj_abs))[n]
                pool.wait_ge(signs_made, n + 1)
                pool.wait_ge(over_half, 2 * (n + 1))
                pool.tensor_tensor(tern[:, :, :], w_sign[:, :, :], over[:, :, :], ALU.mult).then_inc(tern_made, 1)

            def x_stats(g):
                pool.wait_ge(x_averaged, g + 1)
                pool.tensor_tensor(x_var[:, :], x_mean[:, :, 1], eps[:, :], ALU.add).then_inc(x_var_made, 1)
                pool.wait_ge(x_var_made, g + 1)
                need(pool, x_normed, SG * g)
                pool.tensor_tensor(x_rstd[:, :], x_var[:, :], power[:, :], ALU.pow).then_inc(x_rstd_made, 1)

            def x_ctx(g):
                pool.wait_ge(ct_hi_made, g + 1)
                pool.tensor_tensor(ct_lo[:, :, :], c_in[:, :, :], ct_hi[:, :, :].bitcast(F32), ALU.subtract
                                   ).then_inc(ct_lo_made, 1)

            def x_rest(g, m):
                pool.wait_ge(part_high, 2 * DC * g + m + 1)
                need(pool, part_low, 2 * DC * g + m)
                pool.tensor_tensor(rest[:, :], qk[:, m % 2, :], parts[:, m, 0, :], ALU.subtract).then_inc(part_rest, 1)

            def x_low(g, m):
                pool.wait_ge(part_mid, 2 * DC * g + m + 1)
                pool.tensor_tensor(parts[:, m, 2, :], rest[:, :], parts[:, m, 1, :], ALU.subtract
                                   ).then_inc(part_low, 1)

            def bias(g):
                pool.wait_ge(res_loaded, 16 * (g + 1))
                if isinstance(g, int) and g == 0:
                    pool.wait_ge(gates_made, 2)
                for b in range(SG):
                    last = pool.tensor_tensor(x1[:, b, :], x1[:, b, :], bias_o[:, :], ALU.add)
                last.then_inc(res_biased, 1)

            def stats2(g):
                pool.wait_ge(n_averaged, g + 1)
                pool.tensor_tensor(n_var[:, :], n_mean[:, :, 1], eps[:, :], ALU.add).then_inc(n_var_made, 1)
                pool.wait_ge(n_var_made, g + 1)
                need(pool, x1_normed, SG * g)
                pool.tensor_tensor(n_rstd[:, :], n_var[:, :], power[:, :], ALU.pow).then_inc(n_rstd_made, 1)

            def up(g, u):
                pool.wait_ge(relu_made, HC * g + u + 1)
                if u >= 2:
                    pool.wait_ge(sq_lo_made, HC * g + u - 1)
                pool.tensor_tensor(square[:, u % 2, :], relu[:, u % 2, :], relu[:, u % 2, :], ALU.mult
                                   ).then_inc(square_made, 1)

            def down(g, b):
                pool.wait_ge(y_made, SG * g + b + 1)
                pool.tensor_tensor(kept[:, b, :], y[:, b % 2, :], kept[:, b, :], ALU.add).then_inc(out_made, 1)

            pool.memset(power[:, :], -0.5)
            pool.memset(eps[:, :], EPS).then_inc(pool_consts, 1)
            pool.memset(ident[:, :], 0.0).then_inc(pool_consts, 1)
            pool.memset(ident16[:, :], 0.0).then_inc(pool_consts, 1)
            pool.wait_ge(pool_consts, 3)
            for tile in (ident, ident16):
                pool.affine_select(out=tile[:, :], in_=tile[:, :], compare_op=ALU.not_equal, fill=1.0, base=0,
                                   pattern=[[-1, P]], channel_multiplier=1).then_inc(pool_consts, 1)
            pool.memset(vals[:, :, :, :], 1.0).then_inc(pool_consts, 1)
            walk(pool, {"XStats": x_stats, "XCtx": x_ctx, "XHigh": x_rest, "XLow": x_low, "Ones": ones_rows, "Bias": bias, "Stats2": stats2,
                        "Ternary": ternary, "Up": up, "Gain": down})


def kernel(**inputs):
    import numpy as np
    import concourse.bacc as bacc
    from concourse.bass_utils import run_bass_kernel_spmd

    def laid_out(a):
        return np.ascontiguousarray(a)

    take = {name: np.asarray(a) for name, a in inputs.items()}
    arrays = {
        "x": take["x"],
        "ctx_t": take["ctx_1024"].reshape(SEQS * SEQ, D).T,
        "mask": take["mask_BxS2_bk1"],
        "g_xattn": take["g_xattn"],
        "g_ffn": take["g_ffn"],
        "wq": take["L0_xattn_Wq"], "bq": take["L0_xattn_bq"].reshape(DC, P).T,
        "wk": take["L0_xattn_Wk"], "bk": take["L0_xattn_bk"].reshape(DC, P).T,
        "wv": take["L0_xattn_Wv"], "bv": take["L0_xattn_bv"],
        "wo": take["L0_xattn_Wo"], "bo": take["L0_xattn_bo"],
        "fast_b_t": take["L0_ffn_fast_b"].T,
        "w_fc_t": take["L0_ffn_w_fc"].T,
        "w_proj_t": take["L0_ffn_w_proj"].T,
        "u_t8": np.tile(take["L0_ffn_u"].T, (P // RANK, 1)),
        "v": take["L0_ffn_v"],
        "gate": take["L0_ffn_gate"].reshape(1),
    }
    nc = bacc.Bacc("TRN2", target_bir_lowering=False, num_devices=1)
    feed, args = {}, {}
    for name, a in arrays.items():
        a = laid_out(a)
        feed[f"in_{name}"] = a
        args[name] = nc.dram_tensor(f"in_{name}", a.shape, mybir.dt.from_np(a.dtype), kind="ExternalInput").ap()
    args["out"] = nc.dram_tensor("out_x", (SEQS, SEQ, D), F32, kind="ExternalOutput").ap()
    build_block(nc, **args)
    result = run_bass_kernel_spmd(nc, [feed], core_ids=[0])
    return result.results[0]["out_x"]
```
